# Optimizing a Trainium2 kernel written in Bass

```python
import numpy as np
import jax
import jax.numpy as jnp

def _softmax(x, axis=-1):
    return jax.nn.softmax(x, axis=axis)

def _gelu(x):
    return jax.nn.gelu(x, approximate=True)

def _silu(x):
    return jax.nn.silu(x)

def _sigmoid(x):
    return jax.nn.sigmoid(x)

def _layernorm(x, axis=-1, eps=1e-05):
    m = jnp.mean(x, axis=axis, keepdims=True)
    v = jnp.var(x, axis=axis, keepdims=True)
    return (x - m) / jnp.sqrt(v + eps)

def _scatter_add(tgt, idx, src, axis=0):
    return tgt.at[idx].add(src)

def _segment_sum(src, seg, n):
    return jax.ops.segment_sum(src, seg, n)
kernel_name = 'mk_conv_preact_d2_conv_nhwc128_r4_1607e8'

def setup_inputs(seed: int=0):
    np.random.seed(seed)
    _w = jnp.asarray

    def _rec_inputs():
        import jax
        import jax.numpy as jnp
        _gk = jax.random.key(seed)
        x = -0.0003482 + 1 * jax.random.normal(jax.random.fold_in(_gk, 1), (1, 96, 96, 32), jnp.float32)
        return x
    x = _rec_inputs()

    def _L0_conv_setup():
        import jax, jax.numpy as jnp
        import numpy as np
        C_IN = 32
        C_HID = 32
        N_HEADS = 4
        INF = 1000000000.0
        N = 96
        key = jax.random.key(seed)
        ks = jax.random.split(key, 10)
        d = {}
        d['x'] = jax.random.normal(ks[0], (1, N, N, C_IN), dtype=jnp.float32)
        d['mask'] = jnp.ones((1, N, N), dtype=jnp.float32)
        d['ln_gamma'] = jnp.ones((C_IN,), dtype=jnp.float32)
        d['ln_beta'] = jnp.zeros((C_IN,), dtype=jnp.float32)
        d['w_bias'] = jax.random.normal(ks[1], (N_HEADS, C_IN), dtype=jnp.float32) * 0.02
        s = 1.0 / np.sqrt(C_IN)
        d['wq'] = jax.random.normal(ks[2], (N_HEADS, C_HID, C_IN), dtype=jnp.float32) * s
        d['wk'] = jax.random.normal(ks[3], (N_HEADS, C_HID, C_IN), dtype=jnp.float32) * s
        d['wv'] = jax.random.normal(ks[4], (N_HEADS, C_HID, C_IN), dtype=jnp.float32) * s
        d['wg'] = jax.random.normal(ks[5], (N_HEADS, C_HID, C_IN), dtype=jnp.float32) * s
        d['bg'] = jnp.ones((N_HEADS, C_HID), dtype=jnp.float32)
        d['wo'] = jax.random.normal(ks[6], (C_IN, N_HEADS * C_HID), dtype=jnp.float32) * (1.0 / np.sqrt(N_HEADS * C_HID))
        d['bo'] = jnp.zeros((C_IN,), dtype=jnp.float32)
        return d
    _L0_conv_all = _L0_conv_setup()
    _L0_conv_in = {k: v for k, v in _L0_conv_all.items() if k in ('mask', 'ln_gamma', 'ln_beta', 'w_bias', 'wq', 'wk', 'wv', 'wg', 'bg', 'wo', 'bo')}
    del _L0_conv_all

    def _L1_conv_setup():
        import jax, jax.numpy as jnp
        import numpy as np
        C_Z = 32
        C_HIDDEN = 32
        N_RES = 96
        B = 1
        EPS = 1e-05

        def _layernorm(x, w, b):
            mu = jnp.mean(x, axis=-1, keepdims=True)
            var = jnp.mean(jnp.square(x - mu), axis=-1, keepdims=True)
            return (x - mu) * jax.lax.rsqrt(var + EPS) * w + b
        key = jax.random.key(seed)
        ks = jax.random.split(key, 16)
        s_z = 1.0 / np.sqrt(C_Z)
        s_h = 1.0 / np.sqrt(C_HIDDEN)
        return {'z': jax.random.normal(ks[0], (B, N_RES, N_RES, C_Z), dtype=jnp.float32), 'mask': jnp.ones((B, N_RES, N_RES), dtype=jnp.float32), 'ln_in_w': jnp.ones((C_Z,), jnp.float32), 'ln_in_b': jnp.zeros((C_Z,), jnp.float32), 'a_g_w': jax.random.normal(ks[1], (C_HIDDEN, C_Z), jnp.float32) * s_z, 'a_g_b': jnp.zeros((C_HIDDEN,), jnp.float32), 'a_p_w': jax.random.normal(ks[2], (C_HIDDEN, C_Z), jnp.float32) * s_z, 'a_p_b': jnp.zeros((C_HIDDEN,), jnp.float32), 'b_g_w': jax.random.normal(ks[3], (C_HIDDEN, C_Z), jnp.float32) * s_z, 'b_g_b': jnp.zeros((C_HIDDEN,), jnp.float32), 'b_p_w': jax.random.normal(ks[4], (C_HIDDEN, C_Z), jnp.float32) * s_z, 'b_p_b': jnp.zeros((C_HIDDEN,), jnp.float32), 'g_w': jax.random.normal(ks[5], (C_Z, C_Z), jnp.float32) * s_z, 'g_b': jnp.zeros((C_Z,), jnp.float32), 'ln_out_w': jnp.ones((C_HIDDEN,), jnp.float32), 'ln_out_b': jnp.zeros((C_HIDDEN,), jnp.float32), 'z_w': jax.random.normal(ks[6], (C_Z, C_HIDDEN), jnp.float32) * s_h, 'z_b': jnp.zeros((C_Z,), jnp.float32)}
    _L1_conv_all = _L1_conv_setup()
    _L1_conv_in = {k: v for k, v in _L1_conv_all.items() if k in ('mask', 'ln_in_w', 'ln_in_b', 'a_g_w', 'a_g_b', 'a_p_w', 'a_p_b', 'b_g_w', 'b_g_b', 'b_p_w', 'b_p_b', 'g_w', 'g_b', 'ln_out_w', 'ln_out_b', 'z_w', 'z_b')}
    del _L1_conv_all
    return {'x': x, 'L0_conv_mask': _L0_conv_in['mask'], 'L0_conv_ln_gamma': _L0_conv_in['ln_gamma'], 'L0_conv_ln_beta': _L0_conv_in['ln_beta'], 'L0_conv_w_bias': _L0_conv_in['w_bias'], 'L0_conv_wq': _L0_conv_in['wq'], 'L0_conv_wk': _L0_conv_in['wk'], 'L0_conv_wv': _L0_conv_in['wv'], 'L0_conv_wg': _L0_conv_in['wg'], 'L0_conv_bg': _L0_conv_in['bg'], 'L0_conv_wo': _L0_conv_in['wo'], 'L0_conv_bo': _L0_conv_in['bo'], 'L1_conv_mask': _L1_conv_in['mask'], 'L1_conv_ln_in_w': _L1_conv_in['ln_in_w'], 'L1_conv_ln_in_b': _L1_conv_in['ln_in_b'], 'L1_conv_a_g_w': _L1_conv_in['a_g_w'], 'L1_conv_a_g_b': _L1_conv_in['a_g_b'], 'L1_conv_a_p_w': _L1_conv_in['a_p_w'], 'L1_conv_a_p_b': _L1_conv_in['a_p_b'], 'L1_conv_b_g_w': _L1_conv_in['b_g_w'], 'L1_conv_b_g_b': _L1_conv_in['b_g_b'], 'L1_conv_b_p_w': _L1_conv_in['b_p_w'], 'L1_conv_b_p_b': _L1_conv_in['b_p_b'], 'L1_conv_g_w': _L1_conv_in['g_w'], 'L1_conv_g_b': _L1_conv_in['g_b'], 'L1_conv_ln_out_w': _L1_conv_in['ln_out_w'], 'L1_conv_ln_out_b': _L1_conv_in['ln_out_b'], 'L1_conv_z_w': _L1_conv_in['z_w'], 'L1_conv_z_b': _L1_conv_in['z_b']}

def reference(x, L0_conv_mask, L0_conv_ln_gamma, L0_conv_ln_beta, L0_conv_w_bias, L0_conv_wq, L0_conv_wk, L0_conv_wv, L0_conv_wg, L0_conv_bg, L0_conv_wo, L0_conv_bo, L1_conv_mask, L1_conv_ln_in_w, L1_conv_ln_in_b, L1_conv_a_g_w, L1_conv_a_g_b, L1_conv_a_p_w, L1_conv_a_p_b, L1_conv_b_g_w, L1_conv_b_g_b, L1_conv_b_p_w, L1_conv_b_p_b, L1_conv_g_w, L1_conv_g_b, L1_conv_ln_out_w, L1_conv_ln_out_b, L1_conv_z_w, L1_conv_z_b):
    import jax
    import jax.numpy as jnp

    def _L0_conv_ref(x, mask, ln_gamma, ln_beta, w_bias, wq, wk, wv, wg, bg, wo, bo):
        import jax, jax.numpy as jnp
        import numpy as np
        C_IN = 32
        C_HID = 32
        N_HEADS = 4
        INF = 1000000000.0
        N = 96
        mu = jnp.mean(x, axis=-1, keepdims=True)
        var = jnp.var(x, axis=-1, keepdims=True)
        xn = (x - mu) * jax.lax.rsqrt(var + 1e-05) * ln_gamma + ln_beta
        tri_bias = jnp.einsum('bijc,hc->bhij', xn, w_bias)
        mask_bias = (mask - 1.0)[:, :, None, None, :] * INF
        scale = 1.0 / np.sqrt(C_HID)
        q = jnp.einsum('bijc,hdc->bijhd', xn, wq) * scale
        k = jnp.einsum('bijc,hdc->bijhd', xn, wk)
        v = jnp.einsum('bijc,hdc->bijhd', xn, wv)
        scores = jnp.einsum('biqhd,bikhd->bihqk', q, k)
        scores = scores + tri_bias[:, None, :, :, :] + mask_bias
        a = jax.nn.softmax(scores, axis=-1)
        o = jnp.einsum('bihqk,bikhd->biqhd', a, v)
        g = jax.nn.sigmoid(jnp.einsum('bijc,hdc->bijhd', xn, wg) + bg)
        o = o * g
        o = o.reshape(*o.shape[:-2], N_HEADS * C_HID)
        out = jnp.einsum('bijk,ck->bijc', o, wo) + bo
        return out

    def _L1_conv_ref(z, mask, ln_in_w, ln_in_b, a_g_w, a_g_b, a_p_w, a_p_b, b_g_w, b_g_b, b_p_w, b_p_b, g_w, g_b, ln_out_w, ln_out_b, z_w, z_b):
        import jax, jax.numpy as jnp
        import numpy as np
        C_Z = 32
        C_HIDDEN = 32
        N_RES = 96
        B = 1
        EPS = 1e-05

        def _layernorm(x, w, b):
            mu = jnp.mean(x, axis=-1, keepdims=True)
            var = jnp.mean(jnp.square(x - mu), axis=-1, keepdims=True)
            return (x - mu) * jax.lax.rsqrt(var + EPS) * w + b
        m = mask[..., None]
        zn = _layernorm(z, ln_in_w, ln_in_b)
        a = m * jax.nn.sigmoid(jnp.einsum('bijc,hc->bijh', zn, a_g_w) + a_g_b) * (jnp.einsum('bijc,hc->bijh', zn, a_p_w) + a_p_b)
        b = m * jax.nn.sigmoid(jnp.einsum('bijc,hc->bijh', zn, b_g_w) + b_g_b) * (jnp.einsum('bijc,hc->bijh', zn, b_p_w) + b_p_b)
        x = jnp.einsum('bikh,bjkh->bijh', a, b)
        xn = _layernorm(x, ln_out_w, ln_out_b)
        gate = jax.nn.sigmoid(jnp.einsum('bijc,oc->bijo', zn, g_w) + g_b)
        out = gate * (jnp.einsum('bijh,oh->bijo', xn, z_w) + z_b)
        return out

    def _gn(v, G=32, eps=1e-05):
        B_, H_, W_, C_ = v.shape
        g = v.reshape(B_, H_, W_, G, C_ // G)
        m = jnp.mean(g, axis=(1, 2, 4), keepdims=True)
        s = jnp.var(g, axis=(1, 2, 4), keepdims=True)
        return ((g - m) / jnp.sqrt(s + eps)).reshape(v.shape)

    def _ln_c(v, eps=1e-06):
        m = jnp.mean(v, axis=-1, keepdims=True)
        s = jnp.var(v, axis=-1, keepdims=True)
        return (v - m) / jnp.sqrt(s + eps)

    def _ln_t(v, eps=1e-05):
        m = jnp.mean(v, axis=-1, keepdims=True)
        s = jnp.var(v, axis=-1, keepdims=True)
        return (v - m) / jnp.sqrt(s + eps)

    def _to_tokens(v):
        B_, H_, W_, C_ = v.shape
        return v.reshape(B_, H_ * W_, C_)

    def _from_tokens(t, like):
        return t.reshape(like.shape)
    x = x + _L0_conv_ref(_gn(x), L0_conv_mask, L0_conv_ln_gamma, L0_conv_ln_beta, L0_conv_w_bias, L0_conv_wq, L0_conv_wk, L0_conv_wv, L0_conv_wg, L0_conv_bg, L0_conv_wo, L0_conv_bo)
    x = x + _L1_conv_ref(_gn(x), L1_conv_mask, L1_conv_ln_in_w, L1_conv_ln_in_b, L1_conv_a_g_w, L1_conv_a_g_b, L1_conv_a_p_w, L1_conv_a_p_b, L1_conv_b_g_w, L1_conv_b_g_b, L1_conv_b_p_w, L1_conv_b_p_b, L1_conv_g_w, L1_conv_g_b, L1_conv_ln_out_w, L1_conv_ln_out_b, L1_conv_z_w, L1_conv_z_b)
    return x

_drawn_inputs = setup_inputs


def setup_inputs(seed=0):
    import zlib

    import numpy as np

    out = dict(_drawn_inputs(seed))
    spreads = {'L0_conv_ln_gamma': (1.0, 0.2),
     'L0_conv_ln_beta': (0.0, 0.1),
     'L0_conv_bg': (1.0, 0.6),
     'L0_conv_bo': (0.0, 0.1),
     'L1_conv_ln_in_w': (1.0, 0.2),
     'L1_conv_ln_in_b': (0.0, 0.1),
     'L1_conv_a_g_b': (0.0, 0.543),
     'L1_conv_a_p_b': (0.0, 0.1),
     'L1_conv_b_g_b': (0.0, 0.461),
     'L1_conv_b_p_b': (0.0, 0.1),
     'L1_conv_g_b': (0.0, 0.421),
     'L1_conv_ln_out_w': (1.0, 0.2),
     'L1_conv_ln_out_b': (0.0, 0.1),
     'L1_conv_z_b': (0.0, 0.1)}
    factors = {'L0_conv_w_bias': 4.529}
    for name, (base, spread) in spreads.items():
        noise = np.random.default_rng([zlib.crc32(name.encode()), seed]).standard_normal(out[name].shape)
        drawn = base * np.exp(spread * noise) if base else spread * noise
        out[name] = jnp.asarray(drawn.astype(out[name].dtype))
    for name, factor in factors.items():
        out[name] = (out[name] * factor).astype(out[name].dtype)
    return out
```

```python
from contextlib import ExitStack

import concourse.bass as bass
from concourse import mybir

N = 96
C = 32
H = 4
HD = H * C
COPIES = 4
P = 128
TOKENS = N * N
GROUP = 4
GROUPS = N // GROUP
GN = GROUP * N
CHUNKS = 4
CI = N // CHUNKS
PARTS = 3
BODY = 8
SLOTS = 4
GATED = 5
PW = GATED * C
BANK = 512
OUT_BLOCKS = BANK // HD
EPS = 1e-5
INF = 1e9


def triangle_kernel(nc, x, mask0, gamma0, beta0, w_bias, wq, wk, wv, wg, bg, wo, bo,
                    mask1, ln_in_w, ln_in_b, a_g_w, a_g_b, a_p_w, a_p_b, b_g_w, b_g_b, b_p_w, b_p_b,
                    g_w, g_b, ln_out_w, ln_out_b, z_w, z_b, out):
    f32 = mybir.dt.float32
    f32r = mybir.dt.float32r
    ALU = mybir.AluOpType
    ACT = mybir.ActivationFunctionType
    AX = mybir.AxisListType

    ctx = ExitStack()
    with ctx:
        def sb(name, shape, dt=f32):
            return ctx.enter_context(nc.sbuf_tensor(name, shape, dt))

        def sem(name):
            return ctx.enter_context(nc.semaphore(name))

        xt = sb("xt", [N, N, C])
        res = sb("res", [N, N, C])
        work = sb("work", [N, N, C])
        square = sb("square", [N, N, C])
        gate_sb = sb("gate_sb", [N, N, C])
        x_stack = sb("x_stack", [P, N, N], f32r)
        ident = sb("ident", [P, P])
        ones = sb("ones", [N, N])
        ident_r = sb("ident_r", [P, N], f32r)
        lo_w = sb("lo_w", [P, 1])
        wq_in = sb("wq_in", [C, H, C])
        wk_in = sb("wk_in", [C, H, C])
        wv_in = sb("wv_in", [HD, C])
        wg_in = sb("wg_in", [HD, C])
        wb_in = sb("wb_in", [H, C])
        wo_in = sb("wo_in", [C, HD])
        tri_in = sb("tri_in", [HD, C])
        tri_in2 = sb("tri_in2", [C, C])
        wz_in = sb("wz_in", [C, C])
        bg_col = sb("bg_col", [HD, 1])
        bg_half = sb("bg_half", [HD, 1])
        bo_row = sb("bo_row", [N, C])
        gamma_row = sb("gamma_row", [N, C])
        beta_row = sb("beta_row", [N, C])
        gb = sb("gb", [P, 4])
        rows_in = sb("rows_in", [2, PW + C])
        mask_in = sb("mask_in", [N, N])
        mask1_in = sb("mask1_in", [N, N])
        mask_v = sb("mask_v", [N, N])
        mask_hi = sb("mask_hi", [N, N], f32r)
        mask_lo = sb("mask_lo", [N, N], f32r)
        mask_rows = sb("mask_rows", [P, TOKENS])
        mask1_t = sb("mask1_t", [N, N])
        w_tmp = sb("w_tmp", [P, HD])
        w_hi = sb("w_hi", [P, HD], f32r)
        wa_st = sb("wa_st", [P, H, COPIES, C], f32r)
        wv_st = sb("wv_st", [P, HD], f32r)
        wg_st = sb("wg_st", [P, HD], f32r)
        wb_st = sb("wb_st", [P, H], f32r)
        wo_t = sb("wo_t", [HD, C])
        tri_w = sb("tri_w", [P, GROUP, PW])
        tri_z = sb("tri_z", [P, GROUP, C])
        tri_b = sb("tri_b", [P, PW + C], f32r)
        rows_hi = sb("rows_hi", [2, PW + C], f32r)
        lo_row = sb("lo_row", [2, 1])
        ones_r = sb("ones_r", [P, N], f32r)
        part = sb("part", [N, 2, CHUNKS, C])
        total = sb("total", [N, 2, C])
        chan = sb("chan", [N, 6, C])
        tok = sb("tok", [N, 6, N])
        t_buf = sb("t_buf", [P, 2, GN])
        hi_buf = sb("hi_buf", [P, 2, GN], f32r)
        xs = sb("xs", [P, 2, GROUP, N], f32r)
        u_st = sb("u_st", [P, 2, GROUP, H, N], f32r)
        bias_hi = sb("bias_hi", [P, H, N], f32r)
        bias_lo = sb("bias_lo", [P, 2, GROUP, H, N], f32r)
        neg_max = sb("neg_max", [N, BODY, H])
        den = sb("den", [N, BODY, H])
        rden = sb("rden", [N, BODY, H])
        probs = sb("probs", [N, SLOTS, H, N])
        probs_t = sb("probs_t", [P, 2, H, N])
        v_sb = sb("v_sb", [P, 2, GROUP, HD])
        g_sb = sb("g_sb", [HD, 2, GROUP, N])
        o_sb = sb("o_sb", [HD, 2, GROUP, N])

        tri_t = xt
        ab = mask_rows[0:N, 0:2 * C * N].rearrange("k (t h i) -> k t h i", t=2, h=C)
        zn_t = mask_rows[:, 2 * C * N:2 * C * N + GROUPS * N].rearrange("p (b j) -> p b j", j=N)
        parts = mask_rows[0:N, 0:PARTS * CI * COPIES * C].rearrange("j (n i k c) -> j n i k c", n=PARTS, k=COPIES, c=C)
        tn_t = zn_t

        banks = [ctx.enter_context(nc.psum_tensor(f"bank{n}", [P, BANK], f32)) for n in range(8)]
        bank_u = banks[0:2]
        bank_v = banks[2]
        bank_g = banks[3]
        bank_s = banks[4:6]
        bank_t = banks[6]
        bank_o = banks[7]

        x_loaded = [sem(f"x_loaded{n}") for n in range(CHUNKS)]
        weights_loaded = sem("weights_loaded")
        ident_zeroed = sem("ident_zeroed")
        ident_made = sem("ident_made")
        consts_made = sem("consts_made")
        dve_chain = sem("dve_chain")
        zeroed = sem("zeroed")
        prep_mm = sem("prep_mm")
        prep_hi = sem("prep_hi")
        prep_evac = sem("prep_evac")
        mask_split = sem("mask_split")
        mask_rows_ready = sem("mask_rows_ready")
        biased = sem("biased")
        squared = sem("squared")
        summed = sem("summed")
        chan_total = sem("chan_total")
        chan_mm = sem("chan_mm")
        centered = sem("centered")
        var_ready = sem("var_ready")
        root_ready = sem("root_ready")
        normed = sem("normed")
        highs_made = sem("highs_made")
        lows_made = sem("lows_made")
        stack_ready = sem("stack_ready")
        transposed = sem("transposed")
        bias_mm = sem("bias_mm")
        bias_ready = sem("bias_ready")
        xs_ready = [sem(f"xs_ready{n}") for n in range(2)]
        mask_ready = [sem(f"mask_ready{n}") for n in range(2)]
        u_done = sem("u_done")
        u_hi = sem("u_hi")
        u_ready = sem("u_ready")
        v_done = sem("v_done")
        v_ready = sem("v_ready")
        g_done = sem("g_done")
        g_ready = sem("g_ready")
        scores_done = sem("scores_done")
        max_ready = sem("max_ready")
        exp_done = sem("exp_done")
        rden_ready = sem("rden_ready")
        probs_ready = sem("probs_ready")
        t_done = sem("t_done")
        t_ready = sem("t_ready")
        pv_done = sem("pv_done")
        o_ready = sem("o_ready")
        y_done = sem("y_done")
        y_added = sem("y_added")
        block_t = sem("block_t")
        zn_ready = sem("zn_ready")
        proj_done = sem("proj_done")
        gates_ready = sem("gates_ready")
        ab_ready = sem("ab_ready")
        ab_masked = sem("ab_masked")
        tri_done = sem("tri_done")
        tri_copied = sem("tri_copied")
        tri_normed = sem("tri_normed")
        out_t = sem("out_t")
        tn_ready = sem("tn_ready")
        z_done = sem("z_done")
        out_ready = sem("out_ready")
        stored = sem("stored")

        def col(v):
            return v.rearrange("(c o) -> c o", o=1)

        def row(v):
            return v.rearrange("(o c) -> o c", o=1)

        def need(eng, s, value):
            if not isinstance(value, int) or value > 0:
                eng.wait_ge(s, value)

        tri_weights = [a_g_w, b_g_w, g_w, a_p_w]
        tri_biases = [a_g_b, b_g_b, g_b, a_p_b, b_p_b, z_b]
        norm_cols = [ln_in_w, ln_in_b, ln_out_w, ln_out_b]

        U_AHEAD, T_BEHIND, PV_BEHIND = 5, 2, 3
        Y_AFTER = 2 * GROUP + 1
        STEPS = N - GROUP + Y_AFTER + 1

        def live(r, m):
            return 0 <= BODY * r + m < N if isinstance(r, int) else True

        def group(r, m):
            return r * (BODY // GROUP) + m // GROUP

        def par(m):
            return (m // GROUP) % 2

        def run_steps(eng, step):
            for m in range(BODY):
                step(0, m)
            with eng.Fori(1, N // BODY - 1) as r:
                for m in range(BODY):
                    step(r, m)
            for s in range(N - BODY, STEPS):
                step(s // BODY, s % BODY)

        ZEROED = 6
        WEIGHT_DMAS = 16 * (14 + len(tri_weights) + len(tri_biases) + COPIES * len(norm_cols))

        block = ctx.enter_context(nc.Block())

        @block.sync
        def _(sp):
            for n in range(CHUNKS):
                sp.dma_start(xt[:, n * CI:(n + 1) * CI, :],
                             x[0, n * CI:(n + 1) * CI].rearrange("i j c -> j i c")).then_inc(x_loaded[n], 16)
            sp.dma_start(mask1_in[:, :], mask1[0]).then_inc(weights_loaded, 16)
            sp.dma_start(tri_in2[:, :], b_p_w).then_inc(weights_loaded, 16)
            sp.dma_start(wz_in[:, :], z_w).then_inc(weights_loaded, 16)
            for n, w in enumerate(tri_weights):
                sp.dma_start(tri_in[n * C:(n + 1) * C, :], w).then_inc(weights_loaded, 16)
            for n, v in enumerate(tri_biases):
                sp.dma_start(rows_in[:, n * C:(n + 1) * C], row(v).to_broadcast([2, C])).then_inc(weights_loaded, 16)
            sp.wait_ge(mask_split, 2)
            sp.dma_start(mask_rows[N:N + 1, :], mask_hi[:, :].bitcast(f32)).then_inc(mask_rows_ready, 16)
            sp.dma_start(mask_rows[N + 1:N + 2, :], mask_lo[:, :].bitcast(f32)).then_inc(mask_rows_ready, 16)
            sp.wait_ge(mask_rows_ready, 32)
            sp.wait_ge(stack_ready, GROUPS)
            sp.wait_ge(bias_ready, 2)

            def stage(r, m):
                if m % GROUP or not live(r, m):
                    return
                g = group(r, m)
                need(sp, scores_done, GROUP * g - GROUP)
                sp.dma_start(xs[:, par(m)].bitcast(f32),
                             x_stack[:, bass.ds(GROUP * g, GROUP), :].bitcast(f32)).then_inc(xs_ready[par(m)], 16)
                for h in range(H):
                    sp.dma_start(
                        bias_lo[N:N + 2, par(m), :, h, :].bitcast(f32),
                        mask_rows[N:N + 2, bass.ds(GN * g, GN)].rearrange("p (i k) -> p i k", i=GROUP)).then_inc(mask_ready[par(m)], 16)

            run_steps(sp, stage)
            rows = GROUP * OUT_BLOCKS
            for n in range(GROUPS // OUT_BLOCKS):
                sp.wait_ge(out_ready, n + 1)
                sp.dma_start(out[0, n * rows:(n + 1) * rows].rearrange("i j c -> j i c"),
                             square[:, n * rows:(n + 1) * rows, :]).then_inc(stored, 16)
            sp.wait_ge(stored, 16 * (GROUPS // OUT_BLOCKS))

        @block.gpsimd
        def _(pool):
            pool.memset(ident[:, :], 0.0).then_inc(ident_zeroed, 1)
            pool.wait_ge(ident_zeroed, 1)
            pool.affine_select(out=ident[:, :], in_=ident[:, :], compare_op=ALU.not_equal, fill=1.0,
                               base=0, pattern=[[-1, P]], channel_multiplier=1).then_inc(ident_made, 1)
            pool.wait_ge(ident_made, 1)
            zeros = (probs_t[N:P, :, :, :], v_sb[N:P, :, :, :], bias_hi[N:P, :, :].bitcast(f32),
                     bias_lo[N:P, :, :, :, :].bitcast(f32), tri_w[:, :, :], tri_z[:, :, :])
            for n, at in enumerate(zeros):
                pool.memset(at, 0.0).then_inc(zeroed, 1)
                pool.wait_ge(zeroed, n + 1)
            pool.wait_ge(weights_loaded, WEIGHT_DMAS)
            for n in range(CHUNKS):
                pool.wait_ge(x_loaded[n], 16)
                pool.tensor_tensor(res[:, n * CI:(n + 1) * CI, :], xt[:, n * CI:(n + 1) * CI, :],
                                   bo_row[:, None, :].to_broadcast([N, CI, C]), ALU.add).then_inc(biased, 1)

            def normalise(r, m):
                if not live(r, m):
                    return
                pool.wait_ge(rden_ready, BODY * r + m + 1)
                pool.tensor_tensor(probs[:, m % SLOTS], probs[:, m % SLOTS],
                                   rden[:, m, :].unsqueeze(2).to_broadcast([N, H, N]),
                                   ALU.mult).then_inc(probs_ready, 1)

            run_steps(pool, normalise)
            pool.wait_ge(ab_ready, 2 * GROUPS)
            for t in range(2):
                pool.tensor_tensor(ab[:, t], ab[:, t], mask1_t[:, None, :].to_broadcast([N, C, N]),
                                   ALU.mult).then_inc(ab_masked, 1)

        @block.scalar
        def _(act):
            act.dma_start(mask_in[:, :], mask0[0]).then_inc(weights_loaded, 16)
            act.dma_start(wq_in[:, :, :], wq.rearrange("h d c -> d h c")).then_inc(weights_loaded, 16)
            act.dma_start(wk_in[:, :, :], wk.rearrange("h d c -> d h c")).then_inc(weights_loaded, 16)
            act.dma_start(wv_in[:, :], wv.rearrange("h d c -> (h d) c")).then_inc(weights_loaded, 16)
            act.dma_start(wg_in[:, :], wg.rearrange("h d c -> (h d) c")).then_inc(weights_loaded, 16)
            act.dma_start(wb_in[:, :], w_bias).then_inc(weights_loaded, 16)
            act.dma_start(wo_in[:, :], wo).then_inc(weights_loaded, 16)
            act.dma_start(bg_col[:, :], bg.rearrange("h (d o) -> (h d) o", o=1)).then_inc(weights_loaded, 16)
            act.dma_start(bo_row[:, :], row(bo).to_broadcast([N, C])).then_inc(weights_loaded, 16)
            act.dma_start(gamma_row[:, :], row(gamma0).to_broadcast([N, C])).then_inc(weights_loaded, 16)
            act.dma_start(beta_row[:, :], row(beta0).to_broadcast([N, C])).then_inc(weights_loaded, 16)
            for n, v in enumerate(norm_cols):
                for k in range(COPIES):
                    act.dma_start(gb[k * C:(k + 1) * C, n:n + 1], col(v)).then_inc(weights_loaded, 16)

            def squares(k):
                need(act, summed, CHUNKS * k)
                for n in range(CHUNKS):
                    act.wait_ge(centered, CHUNKS * k + n + 1)
                    act.activation(square[:, n * CI:(n + 1) * CI, :], work[:, n * CI:(n + 1) * CI, :],
                                   ACT.Square).then_inc(squared, 1)

            def roots(k, t):
                act.wait_ge(var_ready, k + 1)
                act.activation(t[:, 2], t[:, 1], ACT.Sqrt).then_inc(root_ready, 1)

            squares(0)
            roots(0, chan)
            squares(1)
            roots(1, tok)
            for n in range(CHUNKS + 1):
                if n < CHUNKS:
                    act.wait_ge(normed, n + 1)
                    need(act, transposed, (n - PARTS + 1) * (GROUPS // CHUNKS))
                    act.activation(parts[:, n % PARTS, :, 0:COPIES:2, :].bitcast(f32r),
                                   work[:, n * CI:(n + 1) * CI, None, :].to_broadcast([N, CI, 2, C]),
                                   ACT.Copy).then_inc(highs_made, 1)
                if n:
                    for b in range((n - 1) * (GROUPS // CHUNKS), n * (GROUPS // CHUNKS)):
                        act.wait_ge(transposed, b + 1)
                        act.activation(x_stack[:, b * GROUP:(b + 1) * GROUP, :].rearrange("p i j -> p (i j)"),
                                       banks[b % 4][:, 0:GN], ACT.Copy).then_inc(stack_ready, 1)

            def high_part(r, m):
                m += U_AHEAD
                if not live(r, m):
                    return
                t = BODY * r + m
                act.wait_ge(u_done, t + 1)
                need(act, u_ready, t - 1)
                act.activation(hi_buf[:, m % 2], bank_u[m % 2][:, 0:GN], ACT.Copy).then_inc(u_hi, 1)

            def step_act(r, m):
                high_part(r, m)
                if not live(r, m):
                    return
                s = BODY * r + m
                act.wait_ge(max_ready, s + 1)
                need(act, t_done, s + 1 - SLOTS)
                for h in range(H):
                    e = act.activation(probs[:, m % SLOTS, h], bank_s[m % 2][0:N, h * N:(h + 1) * N],
                                       ACT.Exp, bias=neg_max[:, m, h:h + 1], accum_out=den[:, m, h:h + 1])
                e.then_inc(exp_done, 1)
                if m % GROUP == 1:
                    g = group(r, m)
                    act.wait_ge(g_done, g + 1)
                    need(act, o_ready, g - 1)
                    act.activation(g_sb[:, par(m)].rearrange("p i q -> p (i q)"), bank_g[:, 0:GN], ACT.Tanh,
                                   scale=0.5, bias=bg_half[:, 0:1]).then_inc(g_ready, 1)

            act.wait_ge(bias_ready, 2)
            for m in range(-U_AHEAD, 0):
                high_part(0, m)
            run_steps(act, step_act)

            squares(2)
            roots(2, chan)
            squares(3)
            roots(3, tok)
            for b in range(2 * GROUPS):
                act.wait_ge(proj_done, b + 1)
                need(act, ab_ready, b - 1)
                gates = banks[b % 4][0:N, 0:2 * PW].rearrange("p (i c) -> p i c", i=2)
                act.activation(t_buf[0:N, b % 2, 0:4 * C].rearrange("p (i c) -> p i c", i=2),
                               gates[:, :, 0:2 * C], ACT.Sigmoid).then_inc(gates_ready, 1)
                act.activation(gate_sb[:, 2 * b:2 * b + 2, :], gates[:, :, 2 * C:3 * C],
                               ACT.Sigmoid).then_inc(gates_ready, 1)
            for b in range(C // GROUP):
                act.wait_ge(tri_done, b + 1)
                act.activation(tri_t[:, :, b * GROUP:(b + 1) * GROUP].rearrange("p i h -> p h i"),
                               banks[4 + b % 4][0:N, 0:GN].rearrange("p (h i) -> p h i", h=GROUP),
                               ACT.Copy).then_inc(tri_copied, 1)
            squares(4)
            roots(4, tok)

        @block.vector
        def _(dve):
            chain = [0]

            def link(ins):
                chain[0] += 1
                ins.then_inc(dve_chain, 1)
                dve.wait_ge(dve_chain, chain[0])

            def split(dst, hi, src, lows):
                return dve.scalar_tensor_tensor(dst, hi.bitcast(f32), lows, src, ALU.mult, ALU.add)

            for k in range(COPIES):
                dve.memset(lo_w[k * C:(k + 1) * C, :], -1.0 if k >= COPIES // 2 else 0.0)
            link(dve.memset(ones_r[:, :].bitcast(f32), 0.0))
            link(dve.memset(tri_b[:, :].bitcast(f32), 0.0))
            link(dve.memset(ones_r[0:2, :].bitcast(f32), 1.0))
            dve.memset(ones[:, :], 1.0).then_inc(consts_made, 1)
            dve.wait_ge(ident_made, 1)
            link(dve.tensor_copy(ident_r[:, :], ident[:, 0:N]))
            dve.tensor_scalar(lo_row[:, :], ident[0:2, 1:2], -1.0, None, ALU.mult)
            link(dve.memset(ident_r[N:P, :].bitcast(f32), 0.0))
            dve.memset(ident_r[N:N + 2, :].bitcast(f32), 1.0).then_inc(consts_made, 1)

            def root_of(t, q, k, scale):
                dve.tensor_scalar(t[:, 1], q, scale, EPS, ALU.mult, ALU.add).then_inc(var_ready, 1)
                dve.wait_ge(root_ready, k + 1)
                link(dve.reciprocal(t[:, 3], t[:, 2]))

            def chunk(n):
                return slice(n * CI, (n + 1) * CI)

            def group_norm(src, layer):
                k = 2 * layer
                for n in range(CHUNKS):
                    if not layer:
                        dve.wait_ge(x_loaded[n], 16)
                    ins = dve.tensor_reduce(part[:, 0, n, :], src[:, chunk(n), :].rearrange("p i c -> p c i"),
                                            AX.X, ALU.add)
                link(ins)
                dve.tensor_reduce(total[:, 0, :], part[:, 0].rearrange("p n c -> p c n"), AX.X,
                                  ALU.add).then_inc(chan_total, 1)
                dve.wait_ge(chan_mm, k + 1)
                link(dve.tensor_scalar(chan[:, 0], bank_s[0][0:N, 0:C], 1.0 / TOKENS, None, ALU.mult))
                for n in range(CHUNKS):
                    dve.tensor_tensor(work[:, chunk(n), :], src[:, chunk(n), :],
                                      chan[:, 0:1, :].to_broadcast([N, CI, C]), ALU.subtract).then_inc(centered, 1)
                for n in range(CHUNKS):
                    dve.wait_ge(squared, CHUNKS * k + n + 1)
                    dve.tensor_reduce(part[:, 1, n, :], square[:, chunk(n), :].rearrange("p i c -> p c i"),
                                      AX.X, ALU.add).then_inc(summed, 1)
                dve.wait_ge(summed, CHUNKS * (k + 1))
                dve.tensor_reduce(total[:, 1, :], part[:, 1].rearrange("p n c -> p c n"), AX.X,
                                  ALU.add).then_inc(chan_total, 1)
                dve.wait_ge(chan_mm, k + 2)
                root_of(chan, bank_s[1][0:N, 0:C], k, 1.0 / TOKENS)
                for n in range(CHUNKS):
                    link(dve.tensor_tensor(work[:, chunk(n), :], work[:, chunk(n), :],
                                           chan[:, 3:4, :].to_broadcast([N, CI, C]), ALU.mult))

            def over_deviation(n):
                return dve.tensor_tensor(work[:, chunk(n), :], work[:, chunk(n), :],
                                         tok[:, 3, chunk(n)].unsqueeze(2).to_broadcast([N, CI, C]), ALU.mult)

            def layer_norm(src, k):
                for n in range(CHUNKS):
                    link(dve.tensor_reduce(tok[:, 4, chunk(n)], src[:, chunk(n), :], AX.X, ALU.add))
                    link(dve.tensor_scalar(tok[:, 0, chunk(n)], tok[:, 4, chunk(n)], 1.0 / C, None, ALU.mult))
                    dve.tensor_tensor(work[:, chunk(n), :], src[:, chunk(n), :],
                                      tok[:, 0, chunk(n)].unsqueeze(2).to_broadcast([N, CI, C]),
                                      ALU.subtract).then_inc(centered, 1)
                for n in range(CHUNKS):
                    dve.wait_ge(squared, CHUNKS * k + n + 1)
                    dve.tensor_reduce(tok[:, 5, chunk(n)], square[:, chunk(n), :], AX.X, ALU.add).then_inc(summed, 1)
                dve.wait_ge(summed, CHUNKS * (k + 1))
                root_of(tok, tok[:, 5], k, 1.0 / C)
                if k == 1:
                    return
                for n in range(CHUNKS):
                    over_deviation(n).then_inc(normed, 1)

            dve.wait_ge(weights_loaded, WEIGHT_DMAS)
            link(dve.tensor_scalar(mask_v[:, :], mask_in[:, :], -1.0, INF, ALU.add, ALU.mult))
            dve.tensor_copy(mask_hi[:, :], mask_v[:, :]).then_inc(mask_split, 1)
            dve.wait_ge(mask_split, 1)
            dve.tensor_tensor(mask_lo[:, :], mask_v[:, :], mask_hi[:, :].bitcast(f32),
                              ALU.subtract).then_inc(mask_split, 1)
            dve.tensor_scalar(bg_half[:, :], bg_col[:, :], 0.5, None, ALU.mult)
            for n, (dst, width, by) in enumerate((
                    (None, HD, float(C) ** -0.5), (wv_st, HD, 1.0), (wg_st, HD, 1.0), (wb_st, H, 1.0))):
                dve.wait_ge(prep_mm, n + 1)
                link(dve.tensor_scalar(w_tmp[:, 0:width], banks[n][:, 0:width], by, None, ALU.mult))
                link(dve.tensor_copy(w_hi[:, 0:width], w_tmp[:, 0:width]))
                if dst is None:
                    for k in range(COPIES):
                        link(split(wa_st[:, :, k, :], w_hi[:, :].rearrange("p (h c) -> p h c", h=H),
                                   w_tmp[:, :].rearrange("p (h c) -> p h c", h=H), lo_w[:, 0:1]))
                else:
                    link(split(dst[:, :], w_hi[:, 0:width], w_tmp[:, 0:width], lo_w[:, 0:1]))
            dve.wait_ge(prep_mm, 5)
            dve.tensor_scalar(wo_t[:, :], banks[4][:, 0:C], 0.5, None, ALU.mult)
            dve.tensor_copy(mask1_t[:, :], banks[4][0:N, HD:HD + N])
            dve.wait_ge(prep_mm, 8)
            dve.wait_ge(zeroed, ZEROED)
            for k in range(COPIES):
                at = slice(k * C, (k + 1) * C)
                dve.tensor_copy(tri_w[at, k, 0:HD], banks[5][at, 0:HD])
                dve.tensor_copy(tri_w[at, k, HD:PW], banks[6][at, 0:C])
                dve.tensor_copy(tri_z[at, k, :], banks[7][at, 0:C])
            link(dve.tensor_copy(rows_hi[:, :], rows_in[:, :]))
            split(tri_b[0:2, :], rows_hi[:, :], rows_in[:, :], lo_row[:, 0:1]).then_inc(prep_evac, 1)

            group_norm(xt, 0)
            layer_norm(work, 1)
            for n in range(CHUNKS + 1):
                if n < CHUNKS:
                    link(over_deviation(n))
                    link(dve.tensor_tensor(work[:, chunk(n), :], work[:, chunk(n), :],
                                           gamma_row[:, None, :].to_broadcast([N, CI, C]), ALU.mult))
                    dve.tensor_tensor(work[:, chunk(n), :], work[:, chunk(n), :],
                                      beta_row[:, None, :].to_broadcast([N, CI, C]), ALU.add).then_inc(normed, 1)
                if n:
                    dve.wait_ge(highs_made, n)
                    at = parts[:, (n - 1) % PARTS]
                    dve.tensor_tensor(at[:, :, 1:COPIES:2, :],
                                      work[:, chunk(n - 1), None, :].to_broadcast([N, CI, 2, C]),
                                      at[:, :, 0:COPIES:2, :], ALU.subtract).then_inc(lows_made, 1)
            dve.wait_ge(bias_mm, 1)
            pair_bias = bank_o[0:N, 0:H * N].rearrange("p (k h) -> p h k", h=H)
            link(dve.tensor_copy(bias_hi[0:N, :, :], pair_bias))
            for p in range(2):
                for i in range(GROUP):
                    ins = dve.tensor_tensor(bias_lo[0:N, p, i], pair_bias, bias_hi[0:N].bitcast(f32), ALU.subtract)
                ins.then_inc(bias_ready, 1)

            def low_part(r, m):
                m += U_AHEAD
                if not live(r, m):
                    return
                dve.wait_ge(u_hi, BODY * r + m + 1)
                need(dve, scores_done, GROUP * group(r, m) - GROUP)
                split(u_st[:, par(m), :, m % GROUP, :], hi_buf[:, m % 2].rearrange("p (i k) -> p i k", i=GROUP),
                      bank_u[m % 2][:, 0:GN].rearrange("p (i k) -> p i k", i=GROUP),
                      lo_w[:, 0:1]).then_inc(u_ready, 1)

            def step_dve(r, m):
                s = BODY * r + m
                n = m % GROUP
                if live(r, m):
                    dve.wait_ge(scores_done, s + 1)
                    dve.tensor_reduce(neg_max[:, m, :],
                                      bank_s[m % 2][0:N, 0:H * N].rearrange("p (h k) -> p h k", h=H),
                                      AX.X, ALU.max, negate=True).then_inc(max_ready, 1)
                if n == GROUP - 1 and live(r, m - GROUP):
                    g, p = group(r, m - GROUP), par(m - GROUP)
                    dve.wait_ge(pv_done, GROUP * g + GROUP)
                    dve.wait_ge(g_ready, g + 1)
                    need(dve, y_done, g - 1)
                    dve.scalar_tensor_tensor(o_sb[:, p].rearrange("p i q -> p (i q)"),
                                             g_sb[:, p].rearrange("p i q -> p (i q)"), 1.0, bank_o[:, 0:GN],
                                             ALU.add, ALU.mult).then_inc(o_ready, 1)
                low_part(r, m)
                if live(r, m - 1):
                    dve.wait_ge(exp_done, s)
                    at = (m - 1) % BODY
                    dve.reciprocal(rden[:, at, :], den[:, at, :]).then_inc(rden_ready, 1)
                if n == 2 and live(r, m):
                    g = group(r, m)
                    dve.wait_ge(v_done, g + 1)
                    need(dve, pv_done, GROUP * g - GROUP)
                    dve.tensor_copy(v_sb[0:N, par(m)].rearrange("p i c -> p (i c)"),
                                    bank_v[0:N, :]).then_inc(v_ready, 1)
                if live(r, m - T_BEHIND):
                    dve.wait_ge(t_done, s - T_BEHIND + 1)
                    need(dve, pv_done, s - T_BEHIND - 1)
                    dve.tensor_copy(probs_t[0:N, m % 2].rearrange("p h q -> p (h q)"),
                                    bank_t[0:N, 0:H * N]).then_inc(t_ready, 1)
                if n == 1 and live(r, m - Y_AFTER):
                    g = group(r, m - Y_AFTER)
                    dve.wait_ge(y_done, g + 1)
                    dve.wait_ge(biased, CHUNKS)
                    rows = res[:, bass.ds(GROUP * g, GROUP), :]
                    dve.tensor_tensor(rows, bank_t[0:N, GN:BANK].rearrange("p (i c) -> p i c", c=C), rows,
                                      ALU.add).then_inc(y_added, 1)

            for m in range(-U_AHEAD, 0):
                low_part(0, m)
            run_steps(dve, step_dve)

            dve.wait_ge(y_added, GROUPS)
            group_norm(res, 1)
            layer_norm(work, 3)
            for b in range(GROUPS // GROUP):
                dve.wait_ge(block_t, b + 1)
                dve.tensor_scalar(zn_t[:, b * GROUP:(b + 1) * GROUP, :].rearrange("p b j -> p (b j)"),
                                  banks[b % 4][:, 0:GN], gb[:, 0:1], gb[:, 1:2], ALU.mult, ALU.add).then_inc(zn_ready, 1)
            for b in range(2 * GROUPS):
                dve.wait_ge(gates_ready, 2 * b + 2)
                dve.tensor_tensor(
                    ab[:, :, :, 2 * b:2 * b + 2].rearrange("k t h i -> k i (t h)"),
                    banks[b % 4][0:N, 0:2 * PW].rearrange("p (i c) -> p i c", i=2)[:, :, 3 * C:5 * C],
                    t_buf[0:N, b % 2, 0:4 * C].rearrange("p (i c) -> p i c", i=2), ALU.mult).then_inc(ab_ready, 1)
            dve.wait_ge(tri_copied, C // GROUP)
            layer_norm(tri_t, 4)
            for b in range(GROUPS // GROUP):
                dve.wait_ge(block_t, GROUPS // GROUP + b + 1)
                dve.tensor_scalar(tn_t[:, b * GROUP:(b + 1) * GROUP, :].rearrange("p b j -> p (b j)"),
                                  banks[b % 4][:, 0:GN], gb[:, 2:3], gb[:, 3:4], ALU.mult, ALU.add).then_inc(tn_ready, 1)
            for b in range(GROUPS // OUT_BLOCKS):
                rows = slice(b * GROUP * OUT_BLOCKS, (b + 1) * GROUP * OUT_BLOCKS)
                dve.wait_ge(z_done, b + 1)
                link(dve.tensor_tensor(square[:, rows, :], banks[4 + b % 4][0:N, :].rearrange("p (i c) -> p i c", c=C),
                                       gate_sb[:, rows, :], ALU.mult))
                dve.tensor_tensor(square[:, rows, :], square[:, rows, :], res[:, rows, :],
                                  ALU.add).then_inc(out_ready, 1)

        @block.tensor
        def _(pe):
            pe.wait_ge(weights_loaded, WEIGHT_DMAS)
            pe.wait_ge(ident_made, 1)

            def fourfold(bank, at, w, moving):
                for k in range(COPIES):
                    mm = pe.matmul(bank[k * C:(k + 1) * C, at], w, moving, start=True, stop=True)
                return mm

            for h in range(H):
                mm = fourfold(banks[0], slice(h * C, (h + 1) * C), wk_in[:, h, :], wq_in[:, h, :])
            mm.then_inc(prep_mm, 1)
            fourfold(banks[1], slice(0, HD), wv_in[:, :], ident[:, :]).then_inc(prep_mm, 1)
            fourfold(banks[2], slice(0, HD), wg_in[:, :], ident[:, :]).then_inc(prep_mm, 1)
            fourfold(banks[3], slice(0, H), wb_in[:, :], ident[0:H, 0:H]).then_inc(prep_mm, 1)
            pe.transpose(banks[4][:, 0:C], wo_in[:, :], ident[0:C, 0:C])
            pe.transpose(banks[4][0:N, HD:HD + N], mask1_in[:, :], ident[0:N, 0:N]).then_inc(prep_mm, 1)
            fourfold(banks[5], slice(0, HD), tri_in[:, :], ident[:, :]).then_inc(prep_mm, 1)
            fourfold(banks[6], slice(0, C), tri_in2[:, :], ident[0:C, 0:C]).then_inc(prep_mm, 1)
            fourfold(banks[7], slice(0, C), wz_in[:, :], ident[0:C, 0:C]).then_inc(prep_mm, 1)
            pe.wait_ge(prep_evac, 1)
            pe.wait_ge(zeroed, ZEROED)
            pe.wait_ge(consts_made, 2)

            def channel_sums(layer):
                for t in range(2):
                    pe.wait_ge(chan_total, 2 * layer + t + 1)
                    pe.matmul(bank_s[t][0:N, 0:C], ones[:, :], total[:, t, :], start=True, stop=True).then_inc(chan_mm, 1)

            channel_sums(0)
            for b in range(GROUPS):
                pe.wait_ge(lows_made, b * GROUP // CI + 1)
                need(pe, stack_ready, b - 3)
                for n in range(GROUP):
                    i = b * GROUP + n
                    mm = pe.transpose(banks[b % 4][:, n * N:(n + 1) * N],
                                      parts[:, i // CI % PARTS, i % CI].rearrange("p k c -> p (k c)"),
                                      ident[0:N, 0:N])
                mm.then_inc(transposed, 1)
            pe.wait_ge(stack_ready, GROUPS)
            for k in range(N):
                mm = pe.matmul(bank_o[0:N, k * H:(k + 1) * H], x_stack[:, :, k], wb_st[:, :], start=True, stop=True)
            mm.then_inc(bias_mm, 1)

            def head_projection(r, m):
                m += U_AHEAD
                if not live(r, m):
                    return
                need(pe, u_ready, BODY * r + m - 1)
                pe.matmul(bank_u[m % 2][:, 0:GN], wa_st[:, m % GROUP].rearrange("p k c -> p (k c)"),
                          x_stack[:, bass.ds(GROUP * group(r, m), GROUP), :].rearrange("p i j -> p (i j)"),
                          start=True, stop=True).then_inc(u_done, 1)

            def step_pe(r, m):
                s = BODY * r + m
                n = m % GROUP
                if live(r, m):
                    g, p = group(r, m), par(m)
                    if n == 0:
                        pe.wait_ge(xs_ready[p], 16 * (r + 1))
                        pe.wait_ge(mask_ready[p], 16 * H * (r + 1))
                        pe.wait_ge(u_ready, GROUP * g + GROUP)
                    need(pe, exp_done, s - 1)
                    scores = bank_s[m % 2][0:N, 0:H * N]
                    pe.matmul(scores, xs[:, p, n, :], u_st[:, p, n].rearrange("p h k -> p (h k)"),
                              start=True, stop=False)
                    pe.matmul(scores, ident_r[:, :], bias_hi[:, :, :].rearrange("p h k -> p (h k)"),
                              start=False, stop=False)
                    pe.matmul(scores, ident_r[:, :], bias_lo[:, p, n].rearrange("p h k -> p (h k)"),
                              start=False, stop=True).then_inc(scores_done, 1)
                head_projection(r, m)
                if live(r, m) and n == 0:
                    need(pe, g_ready, g)
                    pe.matmul(bank_g[:, 0:GN], wg_st[:, :], xs[:, p].rearrange("p i q -> p (i q)"),
                              start=True, stop=True).then_inc(g_done, 1)
                    need(pe, v_ready, g)
                    for i in range(GROUP):
                        mm = pe.matmul(bank_v[0:N, i * HD:(i + 1) * HD], xs[:, p, i, :], wv_st[:, :],
                                       start=True, stop=True)
                    mm.then_inc(v_done, 1)
                if n == 1 and live(r, m - Y_AFTER):
                    g, p = group(r, m - Y_AFTER), par(m - Y_AFTER)
                    pe.wait_ge(o_ready, g + 1)
                    need(pe, t_ready, min(s - T_BEHIND, N) if isinstance(r, int) else s - T_BEHIND)
                    for i in range(GROUP):
                        mm = pe.matmul(bank_t[0:N, GN + i * C:GN + (i + 1) * C], o_sb[:, p, i, :], wo_t[:, :],
                                       start=True, stop=True)
                    mm.then_inc(y_done, 1)
                if live(r, m - T_BEHIND):
                    pe.wait_ge(probs_ready, s - T_BEHIND + 1)
                    need(pe, t_ready, s - T_BEHIND)
                    if n == 2 and live(r, m - 1 - Y_AFTER):
                        pe.wait_ge(y_added, group(r, m - 1 - Y_AFTER) + 1)
                    for h in range(H):
                        mm = pe.transpose(bank_t[0:N, h * N:(h + 1) * N], probs[:, (m - T_BEHIND) % SLOTS, h, :],
                                          ident[0:N, 0:N])
                    mm.then_inc(t_done, 1)
                if live(r, m - PV_BEHIND):
                    j = m - PV_BEHIND
                    g, p, i = group(r, j), par(j), j % GROUP
                    pe.wait_ge(t_ready, s - PV_BEHIND + 1)
                    if i == 0:
                        pe.wait_ge(v_ready, g + 1)
                        need(pe, o_ready, g)
                    for h in range(H):
                        mm = pe.matmul(bank_o[h * C:(h + 1) * C, i * N:(i + 1) * N],
                                       v_sb[:, p, i, h * C:(h + 1) * C], probs_t[:, j % 2, h, :],
                                       start=True, stop=True)
                    mm.then_inc(pv_done, 1)

            pe.wait_ge(bias_ready, 2)
            for m in range(-U_AHEAD, 0):
                head_projection(0, m)
            run_steps(pe, step_pe)

            channel_sums(1)

            def block_transposes(done, ready):
                for b in range(GROUPS // GROUP):
                    pe.wait_ge(normed, CHUNKS * done + b * GROUP * GROUP // CI + 1)
                    if b >= 4:
                        pe.wait_ge(ready, b - 3)
                    for n in range(GROUP):
                        i = (b * GROUP + n) * GROUP
                        pe.wait_ge(normed, CHUNKS * done + i // CI + 1)
                        mm = pe.transpose(banks[b % 4][:, n * N:(n + 1) * N],
                                          work[:, i:i + GROUP, :].rearrange("p i c -> p (i c)"), ident[0:N, 0:N])
                    mm.then_inc(block_t, 1)

            block_transposes(1, zn_ready)
            pe.wait_ge(zn_ready, GROUPS // GROUP)
            for b in range(2 * GROUPS):
                need(pe, ab_ready, b - 3)
                proj = banks[b % 4][0:N, 0:2 * PW]
                pe.matmul(proj, ones_r[:, :], tri_b[:, None, 0:PW].to_broadcast([P, 2, PW]), start=True, stop=False)
                pe.matmul(proj, zn_t[:, b // 2, :], tri_w[:, 2 * (b % 2):2 * (b % 2) + 2, :].rearrange("p i c -> p (i c)"),
                          start=False, stop=True).then_inc(proj_done, 1)
            pe.wait_ge(ab_masked, 2)
            for b in range(C // GROUP):
                need(pe, tri_copied, b - 3)
                for n in range(GROUP):
                    h = b * GROUP + n
                    mm = pe.matmul(banks[4 + b % 4][0:N, n * N:(n + 1) * N], ab[:, 1, h, :], ab[:, 0, h, :],
                                   start=True, stop=True)
                mm.then_inc(tri_done, 1)
            block_transposes(2, tn_ready)
            for b in range(GROUPS // OUT_BLOCKS):
                pe.wait_ge(tn_ready, b + 1)
                need(pe, out_ready, b - 3)
                bank = banks[4 + b % 4]
                for n in range(OUT_BLOCKS):
                    at = bank[0:N, n * HD:(n + 1) * HD]
                    pe.matmul(at, ones_r[:, :], tri_b[:, None, PW:PW + C].to_broadcast([P, GROUP, C]),
                              start=True, stop=False)
                    mm = pe.matmul(at, tn_t[:, b * OUT_BLOCKS + n, :], tri_z[:, :, :].rearrange("p i c -> p (i c)"),
                                   start=False, stop=True)
                mm.then_inc(z_done, 1)


_INS = ["x", "L0_conv_mask", "L0_conv_ln_gamma", "L0_conv_ln_beta", "L0_conv_w_bias", "L0_conv_wq",
        "L0_conv_wk", "L0_conv_wv", "L0_conv_wg", "L0_conv_bg", "L0_conv_wo", "L0_conv_bo", "L1_conv_mask",
        "L1_conv_ln_in_w", "L1_conv_ln_in_b", "L1_conv_a_g_w", "L1_conv_a_g_b", "L1_conv_a_p_w",
        "L1_conv_a_p_b", "L1_conv_b_g_w", "L1_conv_b_g_b", "L1_conv_b_p_w", "L1_conv_b_p_b", "L1_conv_g_w",
        "L1_conv_g_b", "L1_conv_ln_out_w", "L1_conv_ln_out_b", "L1_conv_z_w", "L1_conv_z_b"]


def kernel(**inputs):
    import numpy as _np
    import concourse.bacc as _bacc
    from concourse import mybir as _mybir
    from concourse.bass_utils import run_bass_kernel_spmd as _run

    nc = _bacc.Bacc("TRN2", target_bir_lowering=False, num_devices=1)
    arrays, args = {}, []
    for name in _INS:
        a = _np.ascontiguousarray(inputs[name])
        arrays[f"in_{name}"] = a
        args.append(nc.dram_tensor(f"in_{name}", a.shape, _mybir.dt.from_np(a.dtype), kind="ExternalInput").ap())
    args.append(nc.dram_tensor("out_y", inputs["x"].shape, _mybir.dt.float32, kind="ExternalOutput").ap())
    triangle_kernel(nc, *args)
    r = _run(nc, [arrays], core_ids=[0])
    return r.results[0]["out_y"]
```

```python
from contextlib import ExitStack

import concourse.bass as bass
from concourse import mybir

N = 96
C = 32
H = 4
HD = H * C
COPIES = 4
P = 128
TOKENS = N * N
GROUP = 4
BLOCKS = N // GROUP
GN = GROUP * N
CHUNKS = 4
CB = BLOCKS // CHUNKS
BODY = 8
SLOTS = 4
GATES = 3
VALUES = 2
PW = (GATES + VALUES) * C
BANK = 512
QUADS = BLOCKS // 4
STACKED = 3
SB = BLOCKS // STACKED
STORES = 3
EPS = 1e-5
INF = 1e9


def triangle_kernel(nc, x, mask0, gamma0, beta0, w_bias, wq, wk, wv, wg, bg, wo, bo,
                    mask1, ln_in_w, ln_in_b, a_g_w, a_g_b, a_p_w, a_p_b, b_g_w, b_g_b, b_p_w, b_p_b,
                    g_w, g_b, ln_out_w, ln_out_b, z_w, z_b, out):
    f32 = mybir.dt.float32
    f32r = mybir.dt.float32r
    ALU = mybir.AluOpType
    ACT = mybir.ActivationFunctionType
    AX = mybir.AxisListType

    ctx = ExitStack()
    with ctx:
        def sb(name, shape, dt=f32):
            return ctx.enter_context(nc.sbuf_tensor(name, shape, dt))

        def sem(name):
            return ctx.enter_context(nc.semaphore(name))

        xt = sb("xt", [N, BLOCKS, GROUP, C])
        res = sb("res", [N, BLOCKS, GROUP, C])
        work = sb("work", [N, BLOCKS, GROUP, C])
        square = sb("square", [N, BLOCKS, GROUP, C])
        gate_sb = sb("gate_sb", [N, BLOCKS, GROUP, C])
        x_stack = sb("x_stack", [P, GROUP, BLOCKS, N], f32r)
        ident = sb("ident", [P, P])
        ones = sb("ones", [N, N])
        ident_r = sb("ident_r", [P, N], f32r)
        lo_w = sb("lo_w", [P, 1])
        wq_in = sb("wq_in", [C, H, C])
        wk_in = sb("wk_in", [C, H, C])
        wv_in = sb("wv_in", [HD, C])
        wg_in = sb("wg_in", [HD, C])
        wb_in = sb("wb_in", [H, C])
        wo_in = sb("wo_in", [C, HD])
        tri_in = sb("tri_in", [HD, C])
        tri_in2 = sb("tri_in2", [C, C])
        wz_in = sb("wz_in", [C, C])
        bg_col = sb("bg_col", [HD, 1])
        bg_half = sb("bg_half", [HD, 1])
        bo_row = sb("bo_row", [N, C])
        norm_in = sb("norm_in", [6, C])
        norm_wide = sb("norm_wide", [6, C, GROUP])
        gb = sb("gb", [P, 6])
        rows_in = sb("rows_in", [2, PW + C])
        mask_in = sb("mask_in", [N, N])
        mask1_in = sb("mask1_in", [N, N])
        mask_v = sb("mask_v", [N, N])
        mask_parts = sb("mask_parts", [N, 2, N], f32r)
        mask1_t = sb("mask1_t", [N, N])
        w_hi = sb("w_hi", [P, HD], f32r)
        wa_st = sb("wa_st", [P, HD], f32r)
        wv_st = sb("wv_st", [P, HD], f32r)
        wg_st = sb("wg_st", [P, HD], f32r)
        members = sb("members", [P, GROUP])
        wb_diag = sb("wb_diag", [P, H, GROUP])
        w_wide = sb("w_wide", [P, C, GROUP])
        wo_t = sb("wo_t", [HD, C])
        tri_g = sb("tri_g", [P, GROUP, GATES * C])
        tri_v = sb("tri_v", [P, GROUP, VALUES * C])
        tri_z = sb("tri_z", [P, GROUP, C])
        tri_b = sb("tri_b", [P, PW + C], f32r)
        rows_hi = sb("rows_hi", [2, PW + C], f32r)
        lo_row = sb("lo_row", [2, 1])
        ones_r = sb("ones_r", [P, N], f32r)
        part = sb("part", [N, 2, CHUNKS, C])
        total = sb("total", [N, 2, C])
        chan = sb("chan", [N, 6, C])
        tok = sb("tok", [N, 6, BLOCKS, GROUP])
        u_split = sb("u_split", [P, 2, GN], f32r)
        xs = sb("xs", [P, 2, GROUP, N], f32r)
        u_st = sb("u_st", [P, 2, H, GROUP, N], f32r)
        pair_bias = sb("pair_bias", [N, H, N])
        bias_hi = sb("bias_hi", [P, H, N], f32r)
        bias_lo = sb("bias_lo", [P, 2, GROUP, H, N], f32r)
        neg_max = sb("neg_max", [N, BODY, H])
        den = sb("den", [N, BODY, H])
        rden = sb("rden", [N, BODY, H])
        probs = sb("probs", [N, SLOTS, H, N])
        probs_t = sb("probs_t", [P, 2, H, N])
        v_sb = sb("v_sb", [P, 2, GROUP, HD])
        g_sb = sb("g_sb", [HD, 2, GROUP, N])
        o_sb = sb("o_sb", [HD, 2, GROUP, N])
        gates_ab = sb("gates_ab", [N, 2, GROUP, VALUES * C])
        masked = sb("masked", [N, 2, GROUP, VALUES * C])

        SHARED = max(3 * BLOCKS * N, 2 * C * N + BLOCKS * N)
        shared = sb("shared", [P, SHARED])
        x_t = shared[:, 0:BLOCKS * N].rearrange("p (b j) -> p b j", j=N)
        x_parts = shared[:, BLOCKS * N:3 * BLOCKS * N].rearrange("p (t b j) -> p t b j", t=2, j=N)
        ab = shared[0:N, 0:2 * C * N].rearrange("k (t h i) -> k t h i", t=2, h=C)
        zn_t = shared[:, 2 * C * N:2 * C * N + BLOCKS * N].rearrange("p (b j) -> p b j", j=N)
        tn_t = zn_t
        blocks_t = square[:, :, :, :].rearrange("j b f c -> j (b f c)").rearrange("j (b c f) -> j b c f", c=C, f=GROUP)
        tri_t = xt
        mask_flat = gate_sb[C:C + 2 * GROUP].rearrange("p b f c -> p (b f c)")[:, 0:BLOCKS * N].rearrange(
            "p (b k) -> p b k", k=N)
        bias_t = gate_sb[0:GROUP * H].rearrange("p b f c -> p (b f c)")[:, 0:BLOCKS * N].rearrange(
            "p (b j) -> p b j", j=N)

        banks = [ctx.enter_context(nc.psum_tensor(f"bank{n}", [P, BANK], f32)) for n in range(8)]
        bank_uv = banks[0]
        bank_gy = banks[1]
        bank_t = banks[2]
        bank_o = banks[3]
        bank_s = banks[4:8]

        x_loaded = [sem(f"x_loaded{f}") for f in range(GROUP)]
        weights_loaded = sem("weights_loaded")
        weights2_loaded = sem("weights2_loaded")
        ident_zeroed = sem("ident_zeroed")
        ident_made = sem("ident_made")
        zeroed = sem("zeroed")
        consts_made = sem("consts_made")
        dve_chain = sem("dve_chain")
        wq_scaled = sem("wq_scaled")
        widened = sem("widened")
        prep_mm = sem("prep_mm")
        prep_hi = sem("prep_hi")
        prep_split = sem("prep_split")
        prep_copied = sem("prep_copied")
        prep2_mm = sem("prep2_mm")
        prep2_copied = sem("prep2_copied")
        rows_split = sem("rows_split")
        mask_split = sem("mask_split")
        mask_spread = sem("mask_spread")
        biased = sem("biased")
        squared = sem("squared")
        summed = sem("summed")
        chan_total = sem("chan_total")
        chan_mm = sem("chan_mm")
        centered = sem("centered")
        var_ready = sem("var_ready")
        root_ready = sem("root_ready")
        normed = sem("normed")
        transposed = sem("transposed")
        x_t_ready = sem("x_t_ready")
        parts_ready = sem("parts_ready")
        stacked = [sem(f"stacked{n}") for n in range(STACKED)]
        bias_mm = sem("bias_mm")
        bias_copied = sem("bias_copied")
        bias_spread = sem("bias_spread")
        bias_ready = sem("bias_ready")
        bias_copy = sem("bias_copy")
        u_done = sem("u_done")
        u_hi = sem("u_hi")
        u_lo = sem("u_lo")
        staged = [sem(f"staged{n}") for n in range(2)]
        v_done = sem("v_done")
        v_ready = sem("v_ready")
        g_done = sem("g_done")
        g_ready = sem("g_ready")
        scores_done = sem("scores_done")
        max_ready = sem("max_ready")
        exp_done = sem("exp_done")
        rden_ready = sem("rden_ready")
        probs_ready = sem("probs_ready")
        t_done = sem("t_done")
        t_ready = sem("t_ready")
        pv_done = sem("pv_done")
        o_ready = sem("o_ready")
        y_done = sem("y_done")
        y_added = sem("y_added")
        block_t = sem("block_t")
        zn_ready = sem("zn_ready")
        proj_done = sem("proj_done")
        gates_ready = sem("gates_ready")
        ab_ready = sem("ab_ready")
        tri_done = sem("tri_done")
        tri_copied = sem("tri_copied")
        tn_ready = sem("tn_ready")
        z_done = sem("z_done")
        out_ready = sem("out_ready")
        stored = sem("stored")

        def row(v):
            return v.rearrange("(o c) -> o c", o=1)

        def need(eng, s, value):
            if not isinstance(value, int) or value > 0:
                eng.wait_ge(s, value)

        tri_weights = [a_g_w, b_g_w, g_w, a_p_w]
        tri_biases = [a_g_b, b_g_b, g_b, a_p_b, b_p_b, z_b]
        norm_rows = [gamma0, beta0, ln_in_w, ln_in_b, ln_out_w, ln_out_b]

        S_AHEAD, T_BEHIND, PV_BEHIND = 2, 3, 4
        Y_AFTER = 2 * GROUP + 2
        STEPS = N - GROUP + Y_AFTER + 1

        def live(r, m):
            return 0 <= BODY * r + m < N if isinstance(r, int) else True

        def group(r, m):
            return r * (BODY // GROUP) + m // GROUP

        def par(m):
            return (m // GROUP) % 2

        def uses(r, m):
            return r + m // BODY + 1

        def run_steps(eng, step):
            for m in range(BODY):
                step(0, m)
            with eng.Fori(1, N // BODY - 1) as r:
                for m in range(BODY):
                    step(r, m)
            for s in range(N - BODY, STEPS):
                step(s // BODY, s % BODY)

        STAGED = 7
        ZEROED = 4
        WEIGHT_DMAS = 16 * (9 + len(norm_rows))
        WEIGHT2_DMAS = 16 * (3 + len(tri_weights) + len(tri_biases))

        block = ctx.enter_context(nc.Block())

        @block.sync
        def _(sp):
            for f in range(GROUP):
                sp.dma_start(xt[:, :, f, :],
                             x[0, f * BLOCKS:(f + 1) * BLOCKS].rearrange("b j c -> j b c")).then_inc(x_loaded[f], 16)
            for n, v in enumerate(norm_rows):
                sp.dma_start(norm_in[n:n + 1, :], row(v)).then_inc(weights_loaded, 16)
            sp.dma_start(mask1_in[:, :], mask1[0]).then_inc(weights2_loaded, 16)
            sp.dma_start(tri_in2[:, :], b_p_w).then_inc(weights2_loaded, 16)
            sp.dma_start(wz_in[:, :], z_w).then_inc(weights2_loaded, 16)
            for n, w in enumerate(tri_weights):
                sp.dma_start(tri_in[n * C:(n + 1) * C, :], w).then_inc(weights2_loaded, 16)
            for n, v in enumerate(tri_biases):
                sp.dma_start(rows_in[:, n * C:(n + 1) * C], row(v).to_broadcast([2, C])).then_inc(weights2_loaded, 16)
            for t in range(2):
                sp.wait_ge(mask_split, t + 1)
                sp.dma_start(mask_flat[t * GROUP:(t + 1) * GROUP],
                             mask_parts[:, t, :].bitcast(f32)).then_inc(mask_spread, 16)
            for n in range(STACKED):
                at = slice(n * SB, (n + 1) * SB)
                sp.wait_ge(parts_ready, (n + 1) * SB // 4)
                for k in range(COPIES):
                    sp.dma_start(x_stack[k * C:(k + 1) * C, :, at, :].bitcast(f32).rearrange("c f b j -> c f (b j)"),
                                 x_parts[:, k % 2, at, :].rearrange("p b j -> p (b j)")).then_inc(stacked[n], 16)
            sp.wait_ge(bias_copied, QUADS)
            for h in range(H):
                sp.dma_start(pair_bias[:, h, :], bias_t[h * GROUP:(h + 1) * GROUP]).then_inc(bias_spread, 16)
            sp.wait_ge(zeroed, ZEROED)

            def stage(g, p):
                sp.dma_start(xs[:, p].bitcast(f32),
                             x_stack[:, :, bass.ds(g, 1), :].rearrange("p f b j -> p f (b j)").bitcast(f32)
                             ).then_inc(staged[p], 16)
                for t in range(2):
                    sp.dma_start(bias_lo[N + t:N + t + 1, p].bitcast(f32),
                                 mask_flat[t * GROUP:(t + 1) * GROUP, bass.ds(g, 1), :].to_broadcast([GROUP, H, N])
                                 ).then_inc(staged[p], 16)
                for t, split_done in enumerate((u_hi, u_lo)):
                    sp.wait_ge(split_done, g + 1)
                    for k in (2 * t, 2 * t + 1):
                        sp.dma_start(
                            u_st[k * C:(k + 1) * C, p].bitcast(f32).rearrange("c h f k -> c h (f k)"),
                            u_split[:, t].bitcast(f32)).then_inc(staged[p], 16)

            def step_sp(r, m):
                if m % GROUP or not live(r, m + GROUP):
                    return
                g = group(r, m) + 1
                need(sp, scores_done, GROUP * (g - 1))
                stage(g, par(m + GROUP))

            for n in range(STACKED):
                sp.wait_ge(stacked[n], 16 * COPIES)
            sp.wait_ge(mask_spread, 32)
            stage(0, 0)
            run_steps(sp, step_sp)
            for n in range(STORES):
                at = slice(n * BLOCKS // STORES, (n + 1) * BLOCKS // STORES)
                sp.wait_ge(out_ready, (n + 1) * QUADS // STORES)
                for f in range(GROUP):
                    sp.dma_start(out[0, f * BLOCKS:(f + 1) * BLOCKS][at].rearrange("b j c -> j b c"),
                                 square[:, at, f, :]).then_inc(stored, 16)
            sp.wait_ge(stored, 16 * STORES * GROUP)

        @block.gpsimd
        def _(pool):
            pool.memset(ident[:, :], 0.0).then_inc(ident_zeroed, 1)
            pool.wait_ge(ident_zeroed, 1)
            pool.affine_select(out=ident[:, :], in_=ident[:, :], compare_op=ALU.not_equal, fill=1.0,
                               base=0, pattern=[[-1, P]], channel_multiplier=1).then_inc(ident_made, 1)
            pool.wait_ge(ident_made, 1)
            zeros = (probs_t[N:P, :, :, :], v_sb[N:P, :, :, :], bias_hi[N:P, :, :].bitcast(f32),
                     bias_lo[N:P, :, :, :, :].bitcast(f32))
            for n, at in enumerate(zeros):
                pool.memset(at, 0.0).then_inc(zeroed, 1)
                pool.wait_ge(zeroed, n + 1)
            pool.wait_ge(weights_loaded, WEIGHT_DMAS)
            for f in range(GROUP):
                pool.wait_ge(x_loaded[f], 16)
            for n in range(CHUNKS):
                rows = slice(n * CB, (n + 1) * CB)
                pool.tensor_tensor(res[:, rows], xt[:, rows], bo_row[:, None, None, :].to_broadcast([N, CB, GROUP, C]),
                                   ALU.add).then_inc(biased, 1)

            def normalise(r, m):
                if not live(r, m):
                    return
                pool.wait_ge(rden_ready, BODY * r + m + 1)
                pool.tensor_tensor(probs[:, m % SLOTS], probs[:, m % SLOTS],
                                   rden[:, m, :].unsqueeze(2).to_broadcast([N, H, N]),
                                   ALU.mult).then_inc(probs_ready, 1)

            run_steps(pool, normalise)
        @block.scalar
        def _(act):
            act.dma_start(mask_in[:, :], mask0[0]).then_inc(weights_loaded, 16)
            act.dma_start(wq_in[:, :, :], wq.rearrange("h d c -> d h c")).then_inc(weights_loaded, 16)
            act.dma_start(wk_in[:, :, :], wk.rearrange("h d c -> d h c")).then_inc(weights_loaded, 16)
            act.dma_start(wv_in[:, :], wv.rearrange("h d c -> (h d) c")).then_inc(weights_loaded, 16)
            act.dma_start(wg_in[:, :], wg.rearrange("h d c -> (h d) c")).then_inc(weights_loaded, 16)
            act.dma_start(wb_in[:, :], w_bias).then_inc(weights_loaded, 16)
            act.dma_start(wo_in[:, :], wo).then_inc(weights_loaded, 16)
            act.dma_start(bg_col[:, :], bg.rearrange("h (d o) -> (h d) o", o=1)).then_inc(weights_loaded, 16)
            act.dma_start(bo_row[:, :], row(bo).to_broadcast([N, C])).then_inc(weights_loaded, 16)

            def squares(k):
                need(act, summed, CHUNKS * k)
                for n in range(CHUNKS):
                    act.wait_ge(centered, CHUNKS * k + n + 1)
                    act.activation(square[:, n * CB:(n + 1) * CB], work[:, n * CB:(n + 1) * CB],
                                   ACT.Square).then_inc(squared, 1)

            def roots(k, t):
                act.wait_ge(var_ready, k + 1)
                act.activation(t[:, 2], t[:, 1], ACT.Sqrt).then_inc(root_ready, 1)

            act.wait_ge(weights_loaded, WEIGHT_DMAS)
            act.activation(wq_in[:, :, :], wq_in[:, :, :], ACT.Copy, scale=float(C) ** -0.5).then_inc(wq_scaled, 1)
            for n in range(3):
                act.wait_ge(prep_mm, n + 1)
                need(act, prep_split, n)
                act.activation(w_hi[:, :], banks[n][:, 0:HD], ACT.Copy).then_inc(prep_hi, 1)
            act.activation(w_wide[0:H], wb_in[:, :].unsqueeze(2).to_broadcast([H, C, GROUP]), ACT.Copy)
            act.activation(norm_wide[:, :, :], norm_in[:, :].unsqueeze(2).to_broadcast([6, C, GROUP]),
                           ACT.Copy).then_inc(widened, 1)
            act.wait_ge(prep_mm, 4)
            act.wait_ge(consts_made, 3)
            for f in range(GROUP):
                act.activation(wb_diag[:, :, f], banks[5][:, 0:H], ACT.Copy, scale=members[:, f:f + 1])
            act.activation(gb[:, :], banks[5][:, H:H + 6], ACT.Copy)
            act.activation(bg_half[:, :], bg_col[:, :], ACT.Copy, scale=0.5)
            act.activation(wo_t[:, :], banks[6][:, 0:C], ACT.Copy, scale=0.5).then_inc(prep_copied, 1)

            squares(0)
            roots(0, chan)
            squares(1)
            roots(1, tok)
            act.wait_ge(prep_copied, 1)
            for b in range(QUADS):
                act.wait_ge(transposed, b + 1)
                act.activation(x_t[:, 4 * b:4 * b + 4, :].rearrange("p b j -> p (b j)"), banks[b % 4][:, 0:GN],
                               ACT.Identity, scale=gb[:, 0:1], bias=gb[:, 1:2]).then_inc(x_t_ready, 1)
                if b:
                    act.wait_ge(bias_mm, b)
                    act.activation(bias_t[:, 4 * b - 4:4 * b, :].rearrange("p b j -> p (b j)"),
                                   banks[4 + (b - 1) % 4][0:GROUP * H, 0:GN], ACT.Copy).then_inc(bias_copied, 1)
            act.wait_ge(bias_mm, QUADS)
            act.activation(bias_t[:, BLOCKS - 4:BLOCKS, :].rearrange("p b j -> p (b j)"),
                           banks[4 + (QUADS - 1) % 4][0:GROUP * H, 0:GN], ACT.Copy).then_inc(bias_copied, 1)

            def high_part(g, before, times):
                act.wait_ge(u_done, g + 1)
                need(act, staged[before], 16 * STAGED * times)
                act.activation(u_split[:, 0], bank_uv[:, 0:GN], ACT.Copy).then_inc(u_hi, 1)

            def step_act(r, m):
                if not live(r, m):
                    return
                s = BODY * r + m
                act.wait_ge(max_ready, s + 1)
                need(act, t_done, s + 1 - SLOTS)
                for h in range(H):
                    e = act.activation(probs[:, m % SLOTS, h], bank_s[m % 4][0:N, h * N:(h + 1) * N],
                                       ACT.Exp, bias=neg_max[:, m, h:h + 1], accum_out=den[:, m, h:h + 1])
                e.then_inc(exp_done, 1)
                if m % GROUP == 2 and live(r, m + 2 * GROUP):
                    high_part(group(r, m) + 2, par(m + GROUP), uses(r, m + GROUP))
                if m % GROUP == 1:
                    g = group(r, m)
                    act.wait_ge(g_done, g + 1)
                    need(act, o_ready, g - 1)
                    act.activation(g_sb[:, par(m)].rearrange("p i q -> p (i q)"), bank_gy[:, 0:GN], ACT.Tanh,
                                   scale=0.5, bias=bg_half[:, 0:1]).then_inc(g_ready, 1)

            high_part(0, 0, 0)
            act.wait_ge(weights2_loaded, WEIGHT2_DMAS)
            for n, w in enumerate((tri_in[:, :], tri_in2[:, :], wz_in[:, :])):
                rows = w.shape[0]
                if n:
                    act.wait_ge(prep2_mm, n)
                act.activation(w_wide[0:rows], w.unsqueeze(2).to_broadcast([rows, C, GROUP]),
                               ACT.Copy).then_inc(widened, 1)
            act.wait_ge(prep2_mm, 4)
            for f in range(GROUP):
                of = members[:, f:f + 1]
                act.activation(tri_g[:, f, :], banks[3][:, 0:GATES * C], ACT.Copy, scale=of)
                act.activation(tri_v[:, f, 0:C], banks[3][:, GATES * C:HD], ACT.Copy, scale=of)
                act.activation(tri_v[:, f, C:2 * C], banks[4][:, 0:C], ACT.Copy, scale=of)
                act.activation(tri_z[:, f, :], banks[5][:, 0:C], ACT.Copy, scale=of)
            act.activation(mask1_t[:, :], banks[6][0:N, 0:N], ACT.Copy).then_inc(prep2_copied, 1)
            act.wait_ge(bias_ready, 1)
            for i in range(GROUP):
                act.activation(bias_lo[0:N, 1, i], bias_lo[0:N, 0, 0].bitcast(f32), ACT.Copy).then_inc(bias_copy, 1)
            high_part(1, 0, 1)
            run_steps(act, step_act)

            squares(2)
            roots(2, chan)
            squares(3)
            roots(3, tok)
            for b in range(BLOCKS):
                act.wait_ge(proj_done, 2 * b + 1)
                need(act, ab_ready, b - 1)
                gates = banks[b % 2][0:N, 0:GATES * HD].rearrange("p (f c) -> p f c", f=GROUP)
                act.activation(gates_ab[:, b % 2], gates[:, :, 0:2 * C], ACT.Sigmoid).then_inc(gates_ready, 1)
                act.activation(gate_sb[:, b], gates[:, :, 2 * C:3 * C], ACT.Sigmoid).then_inc(gates_ready, 1)
            for b in range(C // GROUP):
                act.wait_ge(tri_done, b + 1)
                act.activation(tri_t[:, :, :, b * GROUP:(b + 1) * GROUP].rearrange("p b f h -> p h f b"),
                               banks[4 + b % 4][0:N, 0:GN].rearrange("p (h f b) -> p h f b", h=GROUP, f=GROUP),
                               ACT.Copy).then_inc(tri_copied, 1)
            squares(4)
            roots(4, tok)

        @block.vector
        def _(dve):
            chain = [0]

            def link(ins):
                chain[0] += 1
                ins.then_inc(dve_chain, 1)
                dve.wait_ge(dve_chain, chain[0])

            def split(dst, hi, src, lows):
                return dve.scalar_tensor_tensor(dst, hi.bitcast(f32), lows, src, ALU.mult, ALU.add)

            for k in range(COPIES):
                dve.memset(lo_w[k * C:(k + 1) * C, :], -1.0 if k >= COPIES // 2 else 0.0)
            link(dve.memset(ones_r[:, :].bitcast(f32), 0.0))
            link(dve.memset(tri_b[:, :].bitcast(f32), 0.0))
            link(dve.memset(ones_r[0:2, :].bitcast(f32), 1.0))
            dve.memset(ones[:, :], 1.0).then_inc(consts_made, 1)
            dve.wait_ge(ident_made, 1)
            link(dve.tensor_copy(ident_r[:, :], ident[:, 0:N]))
            dve.tensor_reduce(members[:, :], ident[:, :].rearrange("p (c f) -> p f c", f=GROUP), AX.X,
                              ALU.add).then_inc(consts_made, 1)
            dve.tensor_scalar(lo_row[:, :], ident[0:2, 1:2], -1.0, None, ALU.mult)
            link(dve.memset(ident_r[N:P, :].bitcast(f32), 0.0))
            dve.memset(ident_r[N:N + 2, :].bitcast(f32), 1.0).then_inc(consts_made, 1)

            def root_of(t, q, k, scale):
                dve.tensor_scalar(t[:, 1], q, scale, EPS, ALU.mult, ALU.add).then_inc(var_ready, 1)
                dve.wait_ge(root_ready, k + 1)
                link(dve.reciprocal(t[:, 3], t[:, 2]))

            def chunk(n):
                return slice(n * CB, (n + 1) * CB)

            def group_norm(src, layer):
                k = 2 * layer
                for n in range(CHUNKS):
                    if layer:
                        at = src[:, chunk(n)].rearrange("p b f c -> p c (b f)")
                    else:
                        dve.wait_ge(x_loaded[n], 16)
                        at = src[:, :, n, :].rearrange("p b c -> p c b")
                    ins = dve.tensor_reduce(part[:, 0, n, :], at, AX.X, ALU.add)
                link(ins)
                dve.tensor_reduce(total[:, 0, :], part[:, 0].rearrange("p n c -> p c n"), AX.X,
                                  ALU.add).then_inc(chan_total, 1)
                dve.wait_ge(chan_mm, k + 1)
                link(dve.tensor_scalar(chan[:, 0], bank_s[0][0:N, 0:C], 1.0 / TOKENS, None, ALU.mult))
                for n in range(CHUNKS):
                    dve.tensor_tensor(work[:, chunk(n)], src[:, chunk(n)], over_rows(chan[:, 0, :]),
                                      ALU.subtract).then_inc(centered, 1)
                for n in range(CHUNKS):
                    dve.wait_ge(squared, CHUNKS * k + n + 1)
                    dve.tensor_reduce(part[:, 1, n, :], square[:, chunk(n)].rearrange("p b f c -> p c (b f)"),
                                      AX.X, ALU.add).then_inc(summed, 1)
                dve.wait_ge(summed, CHUNKS * (k + 1))
                dve.tensor_reduce(total[:, 1, :], part[:, 1].rearrange("p n c -> p c n"), AX.X,
                                  ALU.add).then_inc(chan_total, 1)
                dve.wait_ge(chan_mm, k + 2)
                root_of(chan, bank_s[1][0:N, 0:C], k, 1.0 / TOKENS)
                for n in range(CHUNKS):
                    link(dve.tensor_tensor(work[:, chunk(n)], work[:, chunk(n)], over_rows(chan[:, 3, :]), ALU.mult))

            def over_rows(v):
                return v[:, None, None, :].to_broadcast([N, CB, GROUP, C])

            def over_channels(v):
                return v.unsqueeze(3).to_broadcast([N, CB, GROUP, C])

            def layer_norm(src, k):
                for n in range(CHUNKS):
                    link(dve.tensor_reduce(tok[:, 4, chunk(n)], src[:, chunk(n)], AX.X, ALU.add))
                    link(dve.tensor_scalar(tok[:, 0, chunk(n)], tok[:, 4, chunk(n)], 1.0 / C, None, ALU.mult))
                    dve.tensor_tensor(work[:, chunk(n)], src[:, chunk(n)], over_channels(tok[:, 0, chunk(n)]),
                                      ALU.subtract).then_inc(centered, 1)
                for n in range(CHUNKS):
                    dve.wait_ge(squared, CHUNKS * k + n + 1)
                    dve.tensor_reduce(tok[:, 5, chunk(n)], square[:, chunk(n)], AX.X, ALU.add).then_inc(summed, 1)
                dve.wait_ge(summed, CHUNKS * (k + 1))
                root_of(tok, tok[:, 5], k, 1.0 / C)
                for n in range(CHUNKS):
                    dve.tensor_tensor(blocks_t[:, chunk(n)].rearrange("j b c f -> j b f c"), work[:, chunk(n)],
                                      over_channels(tok[:, 3, chunk(n)]), ALU.mult).then_inc(normed, 1)

            for n, dst in enumerate((wa_st, wv_st, wg_st)):
                dve.wait_ge(prep_hi, n + 1)
                to = dst[:, :] if n else dst[:, :].rearrange("p (c h) -> p h c", h=H)
                at = (lambda v: v) if n else (lambda v: v.rearrange("p (h c) -> p h c", h=H))
                split(to, at(w_hi[:, :]), at(banks[n][:, 0:HD]), lo_w[:, 0:1]).then_inc(prep_split, 1)
            link(dve.tensor_scalar(mask_v[:, :], mask_in[:, :], -1.0, INF, ALU.add, ALU.mult))
            dve.tensor_copy(mask_parts[:, 0], mask_v[:, :]).then_inc(mask_split, 1)
            dve.wait_ge(mask_split, 1)
            dve.tensor_tensor(mask_parts[:, 1], mask_v[:, :], mask_parts[:, 0].bitcast(f32),
                              ALU.subtract).then_inc(mask_split, 1)

            group_norm(xt, 0)
            layer_norm(work, 1)
            for b in range(QUADS):
                at = slice(4 * b, 4 * b + 4)
                dve.wait_ge(x_t_ready, b + 1)
                link(dve.tensor_copy(x_parts[:, 0, at, :].bitcast(f32r), x_t[:, at, :]))
                dve.tensor_tensor(x_parts[:, 1, at, :].bitcast(f32r), x_t[:, at, :], x_parts[:, 0, at, :],
                                  ALU.subtract).then_inc(parts_ready, 1)
            dve.wait_ge(weights2_loaded, WEIGHT2_DMAS)
            link(dve.tensor_copy(rows_hi[:, :], rows_in[:, :]))
            split(tri_b[0:2, :], rows_hi[:, :], rows_in[:, :], lo_row[:, 0:1]).then_inc(rows_split, 1)

            def low_part(g):
                dve.wait_ge(u_hi, g + 1)
                dve.tensor_tensor(u_split[:, 1], bank_uv[:, 0:GN], u_split[:, 0].bitcast(f32),
                                  ALU.subtract).then_inc(u_lo, 1)

            low_part(0)
            dve.wait_ge(bias_spread, 16 * H)
            dve.wait_ge(zeroed, ZEROED)
            link(dve.tensor_copy(bias_hi[0:N], pair_bias[:, :, :]))
            for i in range(GROUP):
                dve.tensor_tensor(bias_lo[0:N, 0, i], pair_bias[:, :, :], bias_hi[0:N].bitcast(f32),
                                  ALU.subtract).then_inc(bias_ready, 1)

            def minus_max(r, m):
                dve.wait_ge(scores_done, BODY * r + m + 1)
                dve.tensor_reduce(neg_max[:, m % BODY, :],
                                  bank_s[m % 4][0:N, 0:H * N].rearrange("p (h k) -> p h k", h=H),
                                  AX.X, ALU.max, negate=True).then_inc(max_ready, 1)

            def step_dve(r, m):
                s = BODY * r + m
                n = m % GROUP
                if live(r, m + 1):
                    minus_max(r, m + 1)
                if n == 0 and live(r, m - 2 * GROUP):
                    g, p = group(r, m - 2 * GROUP), par(m)
                    dve.wait_ge(pv_done, GROUP * g + GROUP)
                    dve.wait_ge(g_ready, g + 1)
                    dve.scalar_tensor_tensor(o_sb[:, p].rearrange("p i q -> p (i q)"),
                                             g_sb[:, p].rearrange("p i q -> p (i q)"), 1.0, bank_o[:, 0:GN],
                                             ALU.add, ALU.mult).then_inc(o_ready, 1)
                if n == 3 and live(r, m + 2 * GROUP):
                    low_part(group(r, m) + 2)
                if n == 1 and live(r, m):
                    g = group(r, m)
                    dve.wait_ge(v_done, g + 1)
                    need(dve, pv_done, GROUP * g - GROUP)
                    dve.tensor_copy(v_sb[0:N, par(m)].rearrange("p i c -> p (i c)"),
                                    bank_uv[0:N, :]).then_inc(v_ready, 1)
                if live(r, m - T_BEHIND):
                    dve.wait_ge(t_done, s - T_BEHIND + 1)
                    need(dve, pv_done, s - T_BEHIND - 1)
                    dve.tensor_copy(probs_t[0:N, (m - T_BEHIND) % 2].rearrange("p h q -> p (h q)"),
                                    bank_t[0:N, 0:H * N]).then_inc(t_ready, 1)
                if live(r, m - 1):
                    dve.wait_ge(exp_done, s)
                    at = (m - 1) % BODY
                    dve.reciprocal(rden[:, at, :], den[:, at, :]).then_inc(rden_ready, 1)
                if n == 2 and live(r, m - Y_AFTER):
                    g = group(r, m - Y_AFTER)
                    dve.wait_ge(y_done, g + 1)
                    dve.wait_ge(biased, CHUNKS)
                    rows = res[:, bass.ds(g, 1)].rearrange("p b f c -> p (b f c)")
                    dve.tensor_tensor(rows, bank_gy[0:N, GN:BANK], rows, ALU.add).then_inc(y_added, 1)

            low_part(1)
            minus_max(0, 0)
            run_steps(dve, step_dve)

            dve.wait_ge(y_added, BLOCKS)
            group_norm(res, 1)
            layer_norm(work, 3)
            for b in range(QUADS):
                dve.wait_ge(block_t, b + 1)
                dve.tensor_scalar(zn_t[:, 4 * b:4 * b + 4, :].rearrange("p b j -> p (b j)"), banks[b % 4][:, 0:GN],
                                  gb[:, 2:3], gb[:, 3:4], ALU.mult, ALU.add).then_inc(zn_ready, 1)
            dve.wait_ge(prep2_copied, 1)
            for b in range(BLOCKS):
                dve.wait_ge(gates_ready, 2 * b + 1)
                link(dve.tensor_tensor(
                    masked[:, b % 2], gates_ab[:, b % 2],
                    mask1_t[:, :].rearrange("k (f b) -> k f b", f=GROUP)[:, :, b:b + 1]
                    .to_broadcast([N, GROUP, VALUES * C]), ALU.mult))
                dve.wait_ge(proj_done, 2 * b + 2)
                dve.tensor_tensor(
                    ab.rearrange("k t h (f b) -> k f (t h) b", f=GROUP)[:, :, :, b],
                    banks[2 + b % 2][0:N, 0:VALUES * HD].rearrange("p (f c) -> p f c", f=GROUP),
                    masked[:, b % 2], ALU.mult).then_inc(ab_ready, 1)
            dve.wait_ge(tri_copied, C // GROUP)
            layer_norm(tri_t, 4)
            for b in range(QUADS):
                dve.wait_ge(block_t, QUADS + b + 1)
                dve.tensor_scalar(tn_t[:, 4 * b:4 * b + 4, :].rearrange("p b j -> p (b j)"), banks[b % 4][:, 0:GN],
                                  gb[:, 4:5], gb[:, 5:6], ALU.mult, ALU.add).then_inc(tn_ready, 1)
            for b in range(QUADS):
                at = slice(4 * b, 4 * b + 4)
                dve.wait_ge(z_done, b + 1)
                link(dve.tensor_tensor(square[:, at], banks[4 + b % 4][0:N, :].rearrange("p (b f c) -> p b f c", f=GROUP, c=C),
                                       gate_sb[:, at], ALU.mult))
                dve.tensor_tensor(square[:, at], square[:, at], res[:, at], ALU.add).then_inc(out_ready, 1)

        @block.tensor
        def _(pe):
            pe.wait_ge(weights_loaded, WEIGHT_DMAS)
            pe.wait_ge(ident_made, 1)

            def fourfold(bank, at, w, moving):
                for k in range(COPIES):
                    mm = pe.matmul(bank[k * C:(k + 1) * C, at], w, moving, start=True, stop=True)
                return mm

            def wide(w):
                return w.rearrange("p c f -> p (c f)")

            pe.wait_ge(wq_scaled, 1)
            for h in range(H):
                mm = fourfold(banks[0], slice(h * C, (h + 1) * C), wk_in[:, h, :], wq_in[:, h, :])
            mm.then_inc(prep_mm, 1)
            fourfold(banks[1], slice(0, HD), wv_in[:, :], ident[:, :]).then_inc(prep_mm, 1)
            fourfold(banks[2], slice(0, HD), wg_in[:, :], ident[:, :]).then_inc(prep_mm, 1)
            pe.wait_ge(widened, 1)
            pe.transpose(banks[5][:, 0:H], wide(w_wide[0:H]), ident[0:H, 0:H])
            pe.transpose(banks[5][:, H:H + 6], wide(norm_wide[:, :, :]), ident[0:6, 0:6])
            pe.transpose(banks[6][:, 0:C], wo_in[:, :], ident[0:C, 0:C]).then_inc(prep_mm, 1)
            pe.wait_ge(consts_made, 3)

            def channel_sums(layer):
                for t in range(2):
                    pe.wait_ge(chan_total, 2 * layer + t + 1)
                    pe.matmul(bank_s[t][0:N, 0:C], ones[:, :], total[:, t, :], start=True, stop=True).then_inc(chan_mm, 1)

            channel_sums(0)

            def block_transposes(done, after, ready, value):
                for b in range(QUADS):
                    pe.wait_ge(normed, CHUNKS * done + (4 * b + 3) // CB + 1)
                    need(pe, ready, value + b - 3 if b >= 4 else 0)
                    for n in range(4):
                        mm = pe.transpose(banks[b % 4][:, n * N:(n + 1) * N],
                                          blocks_t[:, 4 * b + n].rearrange("p c f -> p (c f)"), ident[0:N, 0:N])
                    mm.then_inc(after, 1)

            pe.wait_ge(prep_split, 3)
            pe.wait_ge(prep_copied, 1)
            block_transposes(0, transposed, x_t_ready, 0)
            for b in range(QUADS):
                pe.wait_ge(x_t_ready, b + 1)
                need(pe, bias_copied, b - 3)
                pe.matmul(banks[4 + b % 4][0:GROUP * H, 0:GN], wb_diag[:, :, :].rearrange("p h f -> p (h f)"),
                          x_t[:, 4 * b:4 * b + 4, :].rearrange("p b j -> p (b j)"),
                          start=True, stop=True).then_inc(bias_mm, 1)

            def u_projection(g):
                need(pe, u_lo, g)
                need(pe, v_ready, g - 1)
                pe.matmul(bank_uv[:, 0:GN], wa_st[:, :], x_stack[:, :, bass.ds(g, 1), :].rearrange("p f b j -> p f (b j)"),
                          start=True, stop=True).then_inc(u_done, 1)

            def scores_of(r, m):
                g, p, i = group(r, m), par(m), m % GROUP
                if i == 0:
                    pe.wait_ge(staged[p], 16 * STAGED * uses(r, m))
                need(pe, exp_done, BODY * r + m - 3)
                scores = bank_s[m % 4][0:N, 0:H * N]
                pe.matmul(scores, xs[:, p, i, :], u_st[:, p, :, i, :], start=True, stop=False)
                pe.matmul(scores, ident_r[:, :], bias_hi[:, :, :].rearrange("p h k -> p (h k)"),
                          start=False, stop=False)
                pe.matmul(scores, ident_r[:, :], bias_lo[:, p, i].rearrange("p h k -> p (h k)"),
                          start=False, stop=True).then_inc(scores_done, 1)

            def step_pe(r, m):
                s = BODY * r + m
                n = m % GROUP
                if live(r, m + S_AHEAD):
                    scores_of(r, m + S_AHEAD)
                if live(r, m) and n == 0:
                    g, p = group(r, m), par(m)
                    need(pe, g_ready, g)
                    if live(r, m + 2 - GROUP - Y_AFTER):
                        pe.wait_ge(y_added, group(r, m + 2 - GROUP - Y_AFTER) + 1)
                    pe.matmul(bank_gy[:, 0:GN], wg_st[:, :], xs[:, p].rearrange("p i q -> p (i q)"),
                              start=True, stop=True).then_inc(g_done, 1)
                    pe.wait_ge(u_lo, min(g + 2, BLOCKS) if isinstance(r, int) else g + 2)
                    for i in range(GROUP):
                        mm = pe.matmul(bank_uv[0:N, i * HD:(i + 1) * HD], xs[:, p, i, :], wv_st[:, :],
                                       start=True, stop=True)
                    mm.then_inc(v_done, 1)
                if live(r, m - T_BEHIND):
                    pe.wait_ge(probs_ready, s - T_BEHIND + 1)
                    need(pe, t_ready, s - T_BEHIND)
                    for h in range(H):
                        mm = pe.transpose(bank_t[0:N, h * N:(h + 1) * N], probs[:, (m - T_BEHIND) % SLOTS, h, :],
                                          ident[0:N, 0:N])
                    mm.then_inc(t_done, 1)
                if n == 2 and live(r, m + 2 * GROUP):
                    u_projection(group(r, m) + 2)
                if n == 2 and live(r, m - Y_AFTER):
                    g, p = group(r, m - Y_AFTER), par(m - Y_AFTER)
                    pe.wait_ge(o_ready, g + 1)
                    pe.wait_ge(g_ready, min(group(r, m) + 1, BLOCKS) if isinstance(r, int) else group(r, m) + 1)
                    for i in range(GROUP):
                        mm = pe.matmul(bank_gy[0:N, GN + i * C:GN + (i + 1) * C], o_sb[:, p, i, :], wo_t[:, :],
                                       start=True, stop=True)
                    mm.then_inc(y_done, 1)
                if live(r, m - PV_BEHIND):
                    j = m - PV_BEHIND
                    g, p, i = group(r, j), par(j), j % GROUP
                    pe.wait_ge(t_ready, s - PV_BEHIND + 1)
                    if i == 0:
                        pe.wait_ge(v_ready, g + 1)
                        need(pe, o_ready, g)
                    for h in range(H):
                        mm = pe.matmul(bank_o[h * C:(h + 1) * C, i * N:(i + 1) * N],
                                       v_sb[:, p, i, h * C:(h + 1) * C], probs_t[:, j % 2, h, :],
                                       start=True, stop=True)
                    mm.then_inc(pv_done, 1)

            pe.wait_ge(stacked[0], 16 * COPIES)
            u_projection(0)
            pe.wait_ge(weights2_loaded, WEIGHT2_DMAS)
            pe.wait_ge(bias_copied, QUADS)
            for n, (bank, rows) in enumerate(((banks[3], HD), (banks[4], C), (banks[5], C))):
                pe.wait_ge(widened, n + 2)
                pe.transpose(bank[:, 0:rows], wide(w_wide[0:rows]), ident[0:rows, 0:rows]).then_inc(prep2_mm, 1)
            pe.transpose(banks[6][0:N, 0:N], mask1_in[:, :], ident[0:N, 0:N]).then_inc(prep2_mm, 1)
            pe.wait_ge(prep2_copied, 1)
            pe.wait_ge(zeroed, ZEROED)
            pe.wait_ge(bias_ready, GROUP)
            pe.wait_ge(bias_copy, GROUP)
            for n in range(1, STACKED):
                pe.wait_ge(stacked[n], 16 * COPIES)
            u_projection(1)
            for m in range(S_AHEAD):
                scores_of(0, m)
            run_steps(pe, step_pe)

            channel_sums(1)

            block_transposes(1, block_t, zn_ready, 0)
            pe.wait_ge(zn_ready, QUADS)
            pe.wait_ge(rows_split, 1)
            for b in range(BLOCKS):
                need(pe, gates_ready, 2 * b - 2)
                need(pe, ab_ready, b - 1)
                for bank, w, at, width in ((banks[b % 2], tri_g, 0, GATES * C),
                                           (banks[2 + b % 2], tri_v, GATES * C, VALUES * C)):
                    to = bank[0:N, 0:GROUP * width]
                    pe.matmul(to, ones_r[:, :], tri_b[:, None, at:at + width].to_broadcast([P, GROUP, width]),
                              start=True, stop=False)
                    pe.matmul(to, zn_t[:, b, :], w[:, :, :].rearrange("p f c -> p (f c)"),
                              start=False, stop=True).then_inc(proj_done, 1)
            pe.wait_ge(ab_ready, BLOCKS)
            for b in range(C // GROUP):
                need(pe, tri_copied, b - 3)
                for n in range(GROUP):
                    h = b * GROUP + n
                    mm = pe.matmul(banks[4 + b % 4][0:N, n * N:(n + 1) * N], ab[:, 1, h, :], ab[:, 0, h, :],
                                   start=True, stop=True)
                mm.then_inc(tri_done, 1)
            block_transposes(2, block_t, tn_ready, 0)
            for b in range(QUADS):
                pe.wait_ge(tn_ready, b + 1)
                need(pe, out_ready, b - 3)
                for n in range(4):
                    at = banks[4 + b % 4][0:N, n * HD:(n + 1) * HD]
                    pe.matmul(at, ones_r[:, :], tri_b[:, None, PW:PW + C].to_broadcast([P, GROUP, C]),
                              start=True, stop=False)
                    mm = pe.matmul(at, tn_t[:, 4 * b + n, :], tri_z[:, :, :].rearrange("p f c -> p (f c)"),
                                   start=False, stop=True)
                mm.then_inc(z_done, 1)


_INS = ["x", "L0_conv_mask", "L0_conv_ln_gamma", "L0_conv_ln_beta", "L0_conv_w_bias", "L0_conv_wq",
        "L0_conv_wk", "L0_conv_wv", "L0_conv_wg", "L0_conv_bg", "L0_conv_wo", "L0_conv_bo", "L1_conv_mask",
        "L1_conv_ln_in_w", "L1_conv_ln_in_b", "L1_conv_a_g_w", "L1_conv_a_g_b", "L1_conv_a_p_w",
        "L1_conv_a_p_b", "L1_conv_b_g_w", "L1_conv_b_g_b", "L1_conv_b_p_w", "L1_conv_b_p_b", "L1_conv_g_w",
        "L1_conv_g_b", "L1_conv_ln_out_w", "L1_conv_ln_out_b", "L1_conv_z_w", "L1_conv_z_b"]


def kernel(**inputs):
    import numpy as _np
    import concourse.bacc as _bacc
    from concourse import mybir as _mybir
    from concourse.bass_utils import run_bass_kernel_spmd as _run

    nc = _bacc.Bacc("TRN2", target_bir_lowering=False, num_devices=1)
    arrays, args = {}, []
    for name in _INS:
        a = _np.ascontiguousarray(inputs[name])
        arrays[f"in_{name}"] = a
        args.append(nc.dram_tensor(f"in_{name}", a.shape, _mybir.dt.from_np(a.dtype), kind="ExternalInput").ap())
    args.append(nc.dram_tensor("out_y", inputs["x"].shape, _mybir.dt.float32, kind="ExternalOutput").ap())
    triangle_kernel(nc, *args)
    r = _run(nc, [arrays], core_ids=[0])
    return r.results[0]["out_y"]
```

```python
from contextlib import ExitStack

import concourse.bass as bass
from concourse import mybir

N = 96
C = 32
H = 4
HD = H * C
COPIES = 4
P = 128
TOKENS = N * N
GROUP = 4
BLOCKS = N // GROUP
GN = GROUP * N
CHUNKS = 4
CB = BLOCKS // CHUNKS
BODY = 8
SLOTS = 4
GATES = 3
VALUES = 2
PW = (GATES + VALUES) * C
BANK = 512
QUADS = BLOCKS // 4
TRI_BANKS = C // GROUP
FIRST_STACK = 4
STORES = 3
EPS = 1e-5
INF = 1e9


def triangle_kernel(nc, x, mask0, gamma0, beta0, w_bias, wq, wk, wv, wg, bg, wo, bo,
                    mask1, ln_in_w, ln_in_b, a_g_w, a_g_b, a_p_w, a_p_b, b_g_w, b_g_b, b_p_w, b_p_b,
                    g_w, g_b, ln_out_w, ln_out_b, z_w, z_b, out):
    f32 = mybir.dt.float32
    f32r = mybir.dt.float32r
    ALU = mybir.AluOpType
    ACT = mybir.ActivationFunctionType
    AX = mybir.AxisListType

    ctx = ExitStack()
    with ctx:
        def sb(name, shape, dt=f32):
            return ctx.enter_context(nc.sbuf_tensor(name, shape, dt))

        def sem(name):
            return ctx.enter_context(nc.semaphore(name))

        maps = sb("maps", [N, 3, BLOCKS, GROUP, C])
        xt = maps[:, 0]
        res = sb("res", [N, BLOCKS, GROUP, C])
        work = maps[:, 1]
        square = maps[:, 2]
        gate_sb = sb("gate_sb", [N, BLOCKS, GROUP, C])
        x_stack = sb("x_stack", [P, GROUP, BLOCKS, N], f32r)
        ident = sb("ident", [P, P])
        per_channel = sb("per_channel", [P, C])
        per_member = sb("per_member", [P, GROUP])
        averaging = sb("averaging", [P, GROUP, C])
        centering = sb("centering", [P, C, GROUP])
        centering_r = sb("centering_r", [P, C, GROUP])
        ident_r = sb("ident_r", [P, N], f32r)
        lo_w = sb("lo_w", [P, 1])
        wq_in = sb("wq_in", [C, H, C])
        wk_in = sb("wk_in", [C, H, C])
        wv_in = sb("wv_in", [HD, C])
        wg_in = sb("wg_in", [HD, C])
        wb_in = sb("wb_in", [H, C])
        wo_in = sb("wo_in", [C, HD])
        tri_in = sb("tri_in", [HD, C])
        tri_in2 = sb("tri_in2", [C, C])
        wz_in = sb("wz_in", [C, C])
        bg_col = sb("bg_col", [HD, 1])
        bg_half = sb("bg_half", [HD, 1])
        bo_row = sb("bo_row", [N, C])
        norm_in = sb("norm_in", [6, C])
        norm_wide = sb("norm_wide", [6, C, GROUP])
        gb = sb("gb", [P, 6])
        rows_in = sb("rows_in", [2, PW + C])
        mask_in = sb("mask_in", [N, N])
        mask1_in = sb("mask1_in", [N, N])
        mask_v = sb("mask_v", [N, N])
        mask_parts = sb("mask_parts", [N, 2, H, N])
        mask1_t = sb("mask1_t", [N, N])
        w_all = sb("w_all", [P, 3 * HD + H + 6 + C])
        w_hi = sb("w_hi", [P, 3 * HD], f32r)
        wa_st = sb("wa_st", [P, HD], f32r)
        wv_st = sb("wv_st", [P, HD], f32r)
        wg_st = sb("wg_st", [P, HD], f32r)
        table = sb("table", [1, 4])
        tri_st = sb("tri_st", [P, PW], f32r)
        members = sb("members", [P, GROUP])
        wb_diag = sb("wb_diag", [P, H, GROUP])
        w_wide = sb("w_wide", [H, C, GROUP])
        wo_t = sb("wo_t", [HD, C])
        tri_gv = sb("tri_gv", [P, GROUP, PW])
        tri_z = sb("tri_z", [P, GROUP, C])
        tri_b = sb("tri_b", [P, PW + C], f32r)
        rows_hi = sb("rows_hi", [2, PW + C], f32r)
        lo_row = sb("lo_row", [2, 1])
        ones_r = sb("ones_r", [P, N], f32r)
        stat = sb("stat", [P, QUADS + 6])
        tok = sb("tok", [N, 4, BLOCKS, GROUP])
        u_split = sb("u_split", [P, 2, 2, GN], f32r)
        xs = sb("xs", [P, 2, GROUP, N], f32r)
        u_st = sb("u_st", [P, 2, H, GROUP, N], f32r)
        pair_bias = sb("pair_bias", [N, H, N])
        bias_hi = sb("bias_hi", [P, H, N], f32r)
        bias_lo = sb("bias_lo", [P, 2, GROUP, H, N], f32r)
        neg_max = sb("neg_max", [N, BODY, H])
        den = sb("den", [N, BODY, H])
        rden = sb("rden", [N, BODY, H])
        probs = sb("probs", [N, SLOTS, H, N])
        probs_t = sb("probs_t", [P, 2, H, N])
        v_sb = sb("v_sb", [P, 2, GROUP, HD])
        g_sb = sb("g_sb", [HD, 2, GROUP, N])
        o_sb = sb("o_sb", [HD, 2, GROUP, N])

        w_wide2 = g_sb.rearrange("p s f n -> p (s f n)")[:, 0:3 * C * GROUP].rearrange(
            "p (n c f) -> p n c f", n=3, f=GROUP)

        zn_hi, zn_lo = (v.rearrange("p s f h k -> p (s f h k)").rearrange("p (q n) -> p q n", n=GN)
                        for v in (bias_lo, u_st))

        SHARED = max(3 * BLOCKS * N, 2 * C * N + BLOCKS * N)
        shared = sb("shared", [P, SHARED])
        x_t = shared[:, 0:BLOCKS * N].rearrange("p (b j) -> p b j", j=N)
        raw_t = x_t
        centered_t = shared[:, BLOCKS * N:2 * BLOCKS * N].rearrange("p (b j) -> p b j", j=N)
        squares_t = shared[:, 2 * BLOCKS * N:3 * BLOCKS * N].rearrange("p (b j) -> p b j", j=N)
        x_parts = shared[:, BLOCKS * N:3 * BLOCKS * N].rearrange("p (t b j) -> p t b j", t=2, j=N)
        ab = shared[0:N, 0:2 * C * N].rearrange("k (t h i) -> k t h i", t=2, h=C)
        zn_t = shared[:, 2 * C * N:2 * C * N + BLOCKS * N].rearrange("p (b j) -> p b j", j=N)
        tn_t = zn_t
        blocks_t = square.rearrange("j b f c -> j (b f c)").rearrange("j (b c f) -> j b c f", c=C, f=GROUP)
        squared_d = work.rearrange("j b f c -> j (b f c)").rearrange("j (b c f) -> j b c f", c=C, f=GROUP)
        def by_blocks(v):
            return v.rearrange("j b f c -> j (b f c)").rearrange("j (b c f) -> j b c f", c=C, f=GROUP)

        tri_t, tri_centered, tri_squares = by_blocks(xt), by_blocks(work), by_blocks(square)
        tri_sums = o_sb[0:N].rearrange("j s f n -> j (s f n)")[:, 0:TRI_BANKS * N].rearrange(
            "j (n t) -> j n t", n=TRI_BANKS)
        free = g_sb.rearrange("p s f n -> p (s f n)")
        z_const = free[0:N, 0:HD]
        z_centering = free[:, HD:2 * HD]
        z_scaled = free[:, 2 * HD:3 * HD]
        z_centered = free[:, 3 * HD:4 * HD]
        beta_wide = free[:, 4 * HD:4 * HD + N]
        gate_const = v_sb[0:N].rearrange("j s i c -> j s (i c)").rearrange("j s (b f c) -> j s b f c", f=GROUP, c=C)
        mask_flat = maps[0:2 * GROUP].rearrange("p t b f c -> p (t b f c)").rearrange(
            "p (b n) -> p b n", b=BLOCKS)
        gates_ab, masked = (probs.rearrange("j s h k -> j (s h k)")[:, t * 3 * HD * VALUES:(t + 1) * 3 * HD * VALUES]
                            .rearrange("j (s f c) -> j s f c", s=3, f=GROUP) for t in range(2))
        bias_t = gate_sb[0:GROUP * H].rearrange("p b f c -> p (b f c)")[:, 0:BLOCKS * N].rearrange(
            "p (b j) -> p b j", j=N)

        psum = ctx.enter_context(nc.psum_tensor("psum", [P, 8 * BANK], f32))
        banks = [psum[:, n * BANK:(n + 1) * BANK] for n in range(8)]
        bank_ug = banks[0]
        bank_v = banks[1]
        bank_w = banks[7]
        bank_stat = banks[6]
        bank_t = banks[2]
        bank_o = banks[3]
        bank_s = banks[4:8]

        x_loaded = [sem(f"x_loaded{f}") for f in range(GROUP)]
        weights_loaded = sem("weights_loaded")
        weights2_loaded = sem("weights2_loaded")
        ident_zeroed = sem("ident_zeroed")
        ident_made = sem("ident_made")
        zeroed = sem("zeroed")
        consts_made = sem("consts_made")
        dve_chain = sem("dve_chain")
        wq_scaled = sem("wq_scaled")
        widened = sem("widened")
        scales_ready = sem("scales_ready")
        prep_mm = sem("prep_mm")
        prep_copied = sem("prep_copied")
        prep2_mm = sem("prep2_mm")
        prep2_copied = sem("prep2_copied")
        rows_split = sem("rows_split")
        mask_split = sem("mask_split")
        mask_spread = sem("mask_spread")
        biased = sem("biased")
        stacks_made = sem("stacks_made")
        raw_transposed = sem("raw_transposed")
        raw_copied = sem("raw_copied")
        chan_total = sem("chan_total")
        chan_mm = sem("chan_mm")
        mean_ready = sem("mean_ready")
        chan_centered = sem("chan_centered")
        chan_squared = sem("chan_squared")
        var_ready = sem("var_ready")
        root_ready = sem("root_ready")
        centering_ready = sem("centering_ready")
        d_done = sem("d_done")
        d_squared = sem("d_squared")
        normed = sem("normed")
        centered = sem("centered")
        squared = sem("squared")
        tri_stack_mm = sem("tri_stack_mm")
        tri_stack_copied = sem("tri_stack_copied")
        tri_stack_made = sem("tri_stack_made")
        zn_hi_ready = sem("zn_hi_ready")
        zn_lo_ready = sem("zn_lo_ready")
        gates_masked = sem("gates_masked")
        tri_mean_ready = sem("tri_mean_ready")
        last_centered = sem("last_centered")
        zn_stacked = [sem(f"zn_stacked{q}") for q in range(1, QUADS)]
        z_prepared = sem("z_prepared")
        z_prep_mm = sem("z_prep_mm")
        z_prep_copied = sem("z_prep_copied")
        gate_scaled = sem("gate_scaled")
        const_gated = sem("const_gated")
        root_inverted = sem("root_inverted")
        transposed = sem("transposed")
        x_t_ready = sem("x_t_ready")
        parts_ready = sem("parts_ready")
        stacked = sem("stacked")
        stacked_more = sem("stacked_more")
        bias_mm = sem("bias_mm")
        bias_copied = sem("bias_copied")
        bias_spread = sem("bias_spread")
        bias_ready = sem("bias_ready")
        bias_copy = sem("bias_copy")
        u_done = sem("u_done")
        u_hi = sem("u_hi")
        u_lo = sem("u_lo")
        staged = [sem(f"staged{n}") for n in range(2)]
        v_done = sem("v_done")
        v_ready = sem("v_ready")
        g_done = sem("g_done")
        g_ready = sem("g_ready")
        scores_done = sem("scores_done")
        max_ready = sem("max_ready")
        exp_done = sem("exp_done")
        rden_ready = sem("rden_ready")
        probs_ready = sem("probs_ready")
        t_done = sem("t_done")
        t_ready = sem("t_ready")
        pv_done = sem("pv_done")
        o_ready = sem("o_ready")
        y_done = sem("y_done")
        y_added = sem("y_added")
        block_t = sem("block_t")
        zn_ready = sem("zn_ready")
        proj_done = sem("proj_done")
        gates_ready = sem("gates_ready")
        ab_ready = sem("ab_ready")
        tri_done = sem("tri_done")
        tri_copied = sem("tri_copied")
        tn_ready = sem("tn_ready")
        z_done = sem("z_done")
        out_ready = sem("out_ready")
        stored = sem("stored")

        def row(v):
            return v.rearrange("(o c) -> o c", o=1)

        def need(eng, s, value):
            if not isinstance(value, int) or value > 0:
                eng.wait_ge(s, value)

        tri_weights = [a_g_w, b_g_w, g_w, a_p_w]
        tri_biases = [a_g_b, b_g_b, g_b, a_p_b, b_p_b, z_b]
        norm_rows = [gamma0, beta0, ln_in_w, ln_in_b, ln_out_w, ln_out_b]

        S_AHEAD, T_BEHIND, PV_BEHIND = 2, 3, 4
        U_AHEAD = 3
        Y_AFTER = 2 * GROUP + 1
        STEPS = N - GROUP + Y_AFTER + 2

        def live(r, m):
            return 0 <= BODY * r + m < N if isinstance(r, int) else True

        def group(r, m):
            return r * (BODY // GROUP) + m // GROUP

        def par(m):
            return (m // GROUP) % 2

        def uses(r, m):
            return r + m // BODY + 1

        def run_steps(eng, step):
            for m in range(BODY):
                step(0, m)
            with eng.Fori(1, N // BODY - 2) as r:
                for m in range(BODY):
                    step(r, m)
            for s in range(N - 2 * BODY, STEPS):
                step(s // BODY, s % BODY)

        BIAS_AFTER = 3
        RAW_EARLY = 4

        def raw_bank(q, layer):
            return (q + 4 * layer) % 8

        ZN_AHEAD = 3
        Z_AFTER = 2
        W_ALL = 3 * HD + H + 6 + C
        CONSTS = 4
        STAGED = 6
        ZEROED = 4
        WEIGHT_DMAS = 16 * (9 + len(norm_rows))
        WEIGHT2_DMAS = 16 * (3 + len(tri_weights) + len(tri_biases))

        def projection_banks(b):
            return 2 * (b % 4)

        def projections(b, at):
            n = projection_banks(b)
            pairs = psum[0:N, n * BANK:(n + 2) * BANK].rearrange("p (a x) -> p a x", a=2)[:, :, 0:2 * PW]
            return pairs.rearrange("p a (f c) -> p a f c", f=2)[:, :, :, at]

        def z_bank(q):
            return banks[4 + q] if q < 4 else banks[q - 2]

        def center_chunk(eng, n):
            at = slice(n * CB, (n + 1) * CB)
            return eng.tensor_tensor(tri_centered[:, at], tri_t[:, at],
                                     tok[:, 1, at].unsqueeze(2).to_broadcast([N, CB, C, GROUP]), ALU.subtract)

        def scale_gates(eng, q):
            at = slice(4 * q, 4 * q + 4)
            return eng.tensor_tensor(gate_sb[:, at], gate_sb[:, at],
                                     tok[:, 3, at].unsqueeze(3).to_broadcast([N, 4, GROUP, C]), ALU.mult)

        block = ctx.enter_context(nc.Block())

        @block.sync
        def _(sp):
            for f in range(GROUP):
                sp.dma_start(xt[:, :, f, :],
                             x[0, f * BLOCKS:(f + 1) * BLOCKS].rearrange("b j c -> j b c")).then_inc(x_loaded[f], 16)
            for n, v in enumerate(norm_rows):
                sp.dma_start(norm_in[n:n + 1, :], row(v)).then_inc(weights_loaded, 16)
            sp.dma_start(mask1_in[:, :], mask1[0]).then_inc(weights2_loaded, 16)
            sp.dma_start(tri_in2[:, :], b_p_w).then_inc(weights2_loaded, 16)
            sp.dma_start(wz_in[:, :], z_w).then_inc(weights2_loaded, 16)
            for n, w in enumerate(tri_weights):
                sp.dma_start(tri_in[n * C:(n + 1) * C, :], w).then_inc(weights2_loaded, 16)
            for n, v in enumerate(tri_biases):
                sp.dma_start(rows_in[:, n * C:(n + 1) * C], row(v).to_broadcast([2, C])).then_inc(weights2_loaded, 16)

            def stack(at, blocks, done):
                for k in range(COPIES):
                    sp.dma_start(x_stack[k * C:(k + 1) * C, :, bass.ds(at, blocks), :].bitcast(f32).rearrange("c f b j -> c f (b j)"),
                                 x_parts[:, k % 2, bass.ds(at, blocks), :].rearrange("p b j -> p (b j)")).then_inc(done, 16)

            sp.wait_ge(parts_ready, FIRST_STACK // 4)
            stack(0, FIRST_STACK, stacked)
            sp.wait_ge(mask_split, 3)
            sp.wait_ge(transposed, QUADS)
            sp.wait_ge(biased, CHUNKS)
            for t in range(2):
                sp.dma_start(mask_flat[t * GROUP:(t + 1) * GROUP],
                             mask_parts[:, t].rearrange("i h k -> i (h k)")).then_inc(mask_spread, 16)
            sp.wait_ge(bias_copied, QUADS)
            for h in range(H):
                sp.dma_start(pair_bias[:, h, :], bias_t[h * GROUP:(h + 1) * GROUP]).then_inc(bias_spread, 16)
            sp.wait_ge(zeroed, ZEROED)

            def stage(g, p):
                sp.dma_start(xs[:, p].bitcast(f32),
                             x_stack[:, :, bass.ds(g, 1), :].rearrange("p f b j -> p f (b j)").bitcast(f32)
                             ).then_inc(staged[p], 16)
                sp.dma_start(bias_lo[N:N + 2, p].bitcast(f32).rearrange("t f h k -> t f (h k)"),
                             mask_flat[:, bass.ds(g, 1), :]).then_inc(staged[p], 16)
                for t, split_done in enumerate((u_hi, u_lo)):
                    sp.wait_ge(split_done, g + 1)
                    for k in (2 * t, 2 * t + 1):
                        sp.dma_start(
                            u_st[k * C:(k + 1) * C, p].bitcast(f32).rearrange("c h f k -> c h (f k)"),
                            u_split[:, p, t].bitcast(f32)).then_inc(staged[p], 16)

            def step_sp(r, m):
                if m % GROUP or not live(r, m + GROUP):
                    return
                g = group(r, m) + 1
                need(sp, scores_done, GROUP * (g - 1))
                stage(g, par(m + GROUP))
                if m == 0 and live(r, BODY + GROUP * (FIRST_STACK - 2)):
                    need(sp, stacked_more, 16 * COPIES * r)
                    stack(2 * r + FIRST_STACK, 2, stacked_more)

            sp.wait_ge(stacked, 16 * COPIES)
            sp.wait_ge(mask_spread, 32)
            stage(0, 0)
            sp.wait_ge(parts_ready, QUADS)
            run_steps(sp, step_sp)
            for q in range(1, QUADS):
                for k in range(COPIES):
                    if k < 2:
                        sp.wait_ge(zn_lo_ready if k else zn_hi_ready, q)
                    sp.dma_start(x_stack[k * C:(k + 1) * C, :, 4 * q:4 * q + 4, :].bitcast(f32).rearrange("c f b j -> c f (b j)"),
                                 (zn_lo if k % 2 else zn_hi)[:, q - 1].bitcast(f32)).then_inc(zn_stacked[q - 1], 16)
            for n in range(STORES):
                at = slice(n * BLOCKS // STORES, (n + 1) * BLOCKS // STORES)
                sp.wait_ge(out_ready, (n + 1) * QUADS // STORES)
                for f in range(GROUP):
                    sp.dma_start(out[0, f * BLOCKS:(f + 1) * BLOCKS][at].rearrange("b j c -> j b c"),
                                 square[:, at, f, :]).then_inc(stored, 16)
            sp.wait_ge(stored, 16 * STORES * GROUP)

        @block.gpsimd
        def _(pool):
            pool.memset(ident[:, :], 0.0).then_inc(ident_zeroed, 1)
            pool.wait_ge(ident_zeroed, 1)
            pool.affine_select(out=ident[:, :], in_=ident[:, :], compare_op=ALU.not_equal, fill=1.0,
                               base=0, pattern=[[-1, P]], channel_multiplier=1).then_inc(ident_made, 1)
            pool.wait_ge(ident_made, 1)
            zeros = (probs_t[N:P, :, :, :], v_sb[N:P, :, :, :], bias_hi[N:P, :, :].bitcast(f32),
                     bias_lo[N:P, :, :, :, :].bitcast(f32))
            for n, at in enumerate(zeros):
                pool.memset(at, 0.0).then_inc(zeroed, 1)
                pool.wait_ge(zeroed, n + 1)
            pool.wait_ge(weights_loaded, WEIGHT_DMAS)
            over_heads = mask_v[:, None, :].to_broadcast([N, H, N])
            pool.tensor_scalar(mask_v[:, :], mask_in[:, :], -1.0, INF, ALU.add, ALU.mult).then_inc(mask_split, 1)
            pool.wait_ge(mask_split, 1)
            pool.tensor_copy(mask_parts[:, 0].bitcast(f32r), over_heads).then_inc(mask_split, 1)
            pool.wait_ge(mask_split, 2)
            pool.tensor_tensor(mask_parts[:, 1].bitcast(f32r), over_heads, mask_parts[:, 0],
                               ALU.subtract).then_inc(mask_split, 1)
            for f in range(GROUP):
                pool.wait_ge(x_loaded[f], 16)
            for n in range(CHUNKS):
                rows = slice(n * CB, (n + 1) * CB)
                pool.tensor_tensor(res[:, rows], xt[:, rows], bo_row[:, None, None, :].to_broadcast([N, CB, GROUP, C]),
                                   ALU.add).then_inc(biased, 1)

            def normalise(r, m):
                if not live(r, m):
                    return
                pool.wait_ge(rden_ready, BODY * r + m + 1)
                pool.tensor_tensor(probs[:, m % SLOTS], probs[:, m % SLOTS],
                                   rden[:, m, :].unsqueeze(2).to_broadcast([N, H, N]),
                                   ALU.mult).then_inc(probs_ready, 1)

            run_steps(pool, normalise)
            for q in range(1, QUADS):
                pool.wait_ge(zn_hi_ready, q)
                pool.tensor_tensor(zn_lo[:, q - 1], zn_t[:, 4 * q:4 * q + 4, :].rearrange("p b j -> p (b j)"),
                                   zn_hi[:, q - 1].bitcast(f32), ALU.subtract).then_inc(zn_lo_ready, 1)
            pool.wait_ge(z_prep_copied, 1)
            for q in range(QUADS):
                at = slice(4 * q, 4 * q + 4)
                pool.wait_ge(gates_ready, 2 * (4 * q + 4))
                constant = z_const.rearrange("j (f c) -> j f c", f=GROUP)[:, None, :, :].to_broadcast([N, 4, GROUP, C])
                pool.tensor_tensor(gate_const[:, q % 2], gate_sb[:, at], constant, ALU.mult).then_inc(const_gated, 1)
                pool.wait_ge(const_gated, 2 * q + 1)
                pool.tensor_tensor(res[:, at], res[:, at], gate_const[:, q % 2], ALU.add).then_inc(const_gated, 1)
                pool.wait_ge(const_gated, 2 * q + 2)
            pool.wait_ge(tri_mean_ready, 1)
            for n in range(CHUNKS // 2, CHUNKS):
                center_chunk(pool, n).then_inc(last_centered, 1)
            pool.wait_ge(root_inverted, 1)
            for q in range(1, QUADS):
                scale_gates(pool, q).then_inc(gate_scaled, 1)
        @block.scalar
        def _(act):
            act.dma_start(mask_in[:, :], mask0[0]).then_inc(weights_loaded, 16)
            act.dma_start(wq_in[:, :, :], wq.rearrange("h d c -> d h c")).then_inc(weights_loaded, 16)
            act.dma_start(wk_in[:, :, :], wk.rearrange("h d c -> d h c")).then_inc(weights_loaded, 16)
            act.dma_start(wv_in[:, :], wv.rearrange("h d c -> (h d) c")).then_inc(weights_loaded, 16)
            act.dma_start(wg_in[:, :], wg.rearrange("h d c -> (h d) c")).then_inc(weights_loaded, 16)
            act.dma_start(wb_in[:, :], w_bias).then_inc(weights_loaded, 16)
            act.dma_start(wo_in[:, :], wo).then_inc(weights_loaded, 16)
            act.dma_start(bg_col[:, :], bg.rearrange("h (d o) -> (h d) o", o=1)).then_inc(weights_loaded, 16)
            act.dma_start(bo_row[:, :], row(bo).to_broadcast([N, C])).then_inc(weights_loaded, 16)

            def raw_copy(q, layer):
                act.wait_ge(raw_transposed, QUADS * layer + q + 1)
                act.activation(raw_t[:, 4 * q:4 * q + 4].rearrange("p b j -> p (b j)"),
                               banks[raw_bank(q, layer)][:, 0:GN], ACT.Copy,
                               accum_out=stat[:, q:q + 1]).then_inc(raw_copied, 1)

            def load_table(n, function):
                act.activation(table[:, n:n + 1], ident[0:1, 0:1], function)

            def norm_front(layer):
                for q in range(layer and RAW_EARLY, QUADS):
                    raw_copy(q, layer)
                if not layer:
                    first_weights()
                act.wait_ge(mean_ready, layer + 1)
                act.activation(squares_t, raw_t, ACT.Square, bias=stat[:, QUADS + 1:QUADS + 2],
                               accum_out=stat[:, QUADS + 2:QUADS + 3]).then_inc(chan_squared, 1)
                if not layer:
                    first_copies()
                act.wait_ge(var_ready, 2 * layer + 1)
                act.activation(stat[:, QUADS + 4:QUADS + 5], stat[:, QUADS + 3:QUADS + 4],
                               ACT.Sqrt).then_inc(root_ready, 1)
                for q in range(QUADS):
                    act.wait_ge(d_done, QUADS * layer + q + 1)
                    act.activation(squared_d[:, 4 * q:4 * q + 4].rearrange("j b c f -> j (b c f)"),
                                   banks[q][0:N, :], ACT.Square).then_inc(d_squared, 1)
                    if not layer and q < GROUP:
                        second_diagonals(q)
                if layer:
                    act.wait_ge(z_prep_mm, 1)
                    act.activation(z_centered, bank_w[:, 0:HD], ACT.Copy)
                    act.activation(z_const, bank_w[0:N, HD:2 * HD], ACT.Copy).then_inc(z_prep_copied, 1)
                act.wait_ge(var_ready, 2 * layer + 2)
                act.activation(tok[:, 2], tok[:, 1], ACT.Sqrt).then_inc(root_ready, 1)

            def first_weights():
                act.wait_ge(weights_loaded, WEIGHT_DMAS)
                act.activation(wq_in[:, :, :], wq_in[:, :, :], ACT.Copy, scale=float(C) ** -0.5).then_inc(wq_scaled, 1)
                act.activation(w_wide[0:H], wb_in[:, :].unsqueeze(2).to_broadcast([H, C, GROUP]), ACT.Copy)
                act.activation(norm_wide[:, :, :], norm_in[:, :].unsqueeze(2).to_broadcast([6, C, GROUP]),
                               ACT.Copy).then_inc(widened, 1)

            def first_copies():
                act.wait_ge(prep_mm, 1)
                act.activation(w_all[:, :], bank_w[:, 0:W_ALL], ACT.Copy).then_inc(prep_copied, 1)
                act.wait_ge(weights2_loaded, WEIGHT2_DMAS)
                for n, w in enumerate((tri_in[:, :], tri_in2[:, :], wz_in[:, :])):
                    rows = w.shape[0]
                    act.activation(w_wide2[0:rows, n], w.unsqueeze(2).to_broadcast([rows, C, GROUP]),
                                   ACT.Copy).then_inc(widened, 1)

            def second_diagonals(f):
                of = members[:, f:f + 1]
                act.wait_ge(prep2_mm, 1)
                act.activation(tri_gv[:, f, :], bank_w[:, 0:PW], ACT.Copy, scale=of)
                act.activation(tri_z[:, f, :], bank_w[:, PW:PW + C], ACT.Copy, scale=of)
                if f == GROUP - 1:
                    act.activation(mask1_t[:, :], bank_w[0:N, PW + C:PW + C + N], ACT.Copy).then_inc(prep2_copied, 1)

            act.wait_ge(ident_made, 1)
            load_table(0, ACT.Sqrt)
            norm_front(0)
            load_table(1, ACT.Exp)
            act.wait_ge(tri_stack_mm, 1)
            act.wait_ge(stacks_made, 3)
            act.activation(w_all[:, 0:PW], bank_w[:, 0:PW], ACT.Copy).then_inc(tri_stack_copied, 1)
            act.wait_ge(consts_made, CONSTS)
            act.wait_ge(prep_copied, 1)
            for f in range(GROUP):
                act.activation(wb_diag[:, :, f], w_all[:, 3 * HD:3 * HD + H], ACT.Copy, scale=members[:, f:f + 1])
            act.activation(gb[:, :], w_all[:, 3 * HD + H:3 * HD + H + 6], ACT.Copy).then_inc(scales_ready, 1)
            act.wait_ge(scales_ready, 1)
            for b in range(QUADS + BIAS_AFTER):
                if b < QUADS:
                    act.wait_ge(transposed, b + 1)
                    act.activation(x_t[:, 4 * b:4 * b + 4, :].rearrange("p b j -> p (b j)"), banks[6 + b % 2][:, 0:GN],
                                   ACT.Identity, scale=gb[:, 0:1], bias=gb[:, 1:2]).then_inc(x_t_ready, 1)
                if b >= BIAS_AFTER:
                    q = b - BIAS_AFTER
                    act.wait_ge(bias_mm, q + 1)
                    act.activation(bias_t[:, 4 * q:4 * q + 4, :].rearrange("p b j -> p (b j)"),
                                   banks[q][0:GROUP * H, 0:GN], ACT.Copy).then_inc(bias_copied, 1)

            def high_part(g, p):
                act.wait_ge(u_done, g + 1)
                act.activation(u_split[:, p, 0], bank_ug[:, 0:GN], ACT.Copy).then_inc(u_hi, 1)

            def step_act(r, m):
                if not live(r, m):
                    if BODY * r + m - N < RAW_EARLY:
                        raw_copy(BODY * r + m - N, 1)
                    return
                s = BODY * r + m
                act.wait_ge(max_ready, s + 1)
                need(act, t_done, s + 1 - SLOTS)
                for h in range(H):
                    e = act.activation(probs[:, m % SLOTS, h], bank_s[m % 4][0:N, h * N:(h + 1) * N],
                                       ACT.Exp, bias=neg_max[:, m, h:h + 1], accum_out=den[:, m, h:h + 1])
                e.then_inc(exp_done, 1)
                if m % GROUP == 3 and live(r, m + U_AHEAD * GROUP):
                    act.wait_ge(staged[par(m + GROUP)], 16 * STAGED * uses(r, m + GROUP))
                    high_part(group(r, m) + U_AHEAD, par(m + GROUP))
                if m % GROUP == 1:
                    gate_of(group(r, m), par(m))

            def gate_of(g, p):
                act.wait_ge(g_done, g + 1)
                act.activation(g_sb[:, p].rearrange("p i q -> p (i q)"), bank_ug[:, 0:GN], ACT.Tanh,
                               scale=0.5, bias=bg_half[:, 0:1]).then_inc(g_ready, 1)

            high_part(0, 0)
            act.activation(bg_half[:, :], bg_col[:, :], ACT.Copy, scale=0.5)
            act.activation(wo_t[:, :], w_all[:, 3 * HD + H + 6:W_ALL], ACT.Copy, scale=0.5)
            high_part(1, 1)
            act.wait_ge(bias_ready, 1)
            act.activation(bias_lo[0:N, 1], bias_lo[0:N, 0, 0:1].bitcast(f32).to_broadcast([N, GROUP, H, N]),
                           ACT.Copy).then_inc(bias_copy, 1)
            act.wait_ge(staged[0], 16 * STAGED)
            high_part(2, 0)
            run_steps(act, step_act)
            load_table(2, ACT.Sqrt)

            norm_front(1)
            load_table(3, ACT.Sigmoid)

            def zn_copy(q):
                act.wait_ge(transposed, QUADS + q + 1)
                act.activation(zn_t[:, 4 * q:4 * q + 4, :].rearrange("p b j -> p (b j)"), banks[6 + q % 2][:, 0:GN],
                               ACT.Identity, scale=gb[:, 2:3], bias=gb[:, 3:4]).then_inc(zn_ready, 1)

                if q:
                    act.wait_ge(zn_ready, q + 1)
                    act.activation(zn_hi[:, q - 1], zn_t[:, 4 * q:4 * q + 4, :].rearrange("p b j -> p (b j)"),
                                   ACT.Copy).then_inc(zn_hi_ready, 1)

            for q in range(ZN_AHEAD):
                zn_copy(q)
            for b in range(BLOCKS):
                if 0 < b <= QUADS - ZN_AHEAD:
                    zn_copy(ZN_AHEAD + b - 1)
                act.wait_ge(proj_done, b + 1)
                need(act, gates_masked, b - 2)
                act.activation(gates_ab[:, b % 3].rearrange("j (a f) c -> j a f c", a=2),
                               projections(b, slice(0, VALUES * C)), ACT.Sigmoid).then_inc(gates_ready, 1)
                act.activation(gate_sb[:, b].rearrange("j (a f) c -> j a f c", a=2),
                               projections(b, slice(VALUES * C, GATES * C)), ACT.Sigmoid).then_inc(gates_ready, 1)
            for b in range(TRI_BANKS):
                act.wait_ge(tri_done, b + 1)
                act.activation(tri_t[:, :, b * GROUP:(b + 1) * GROUP, :].rearrange("p b h f -> p h f b"),
                               banks[4 + b % 4][0:N, 0:GN].rearrange("p (h f b) -> p h f b", h=GROUP, f=GROUP),
                               ACT.Copy).then_inc(tri_copied, 1)
            for q in range(QUADS):
                act.wait_ge(block_t, q + 1)
                act.activation(tn_t[:, 4 * q:4 * q + 4, :].rearrange("p b j -> p (b j)"), banks[q % 4][:, 0:GN],
                               ACT.Copy).then_inc(tn_ready, 1)
                n = q - 1
                if 0 <= n < CHUNKS:
                    if n < CHUNKS // 2:
                        act.wait_ge(centered, n + 1)
                    else:
                        act.wait_ge(last_centered, n + 1 - CHUNKS // 2)
                    act.activation(tri_squares[:, n * CB:(n + 1) * CB], tri_centered[:, n * CB:(n + 1) * CB],
                                   ACT.Square).then_inc(squared, 1)
            act.wait_ge(var_ready, 5)
            act.activation(tok[:, 2], tok[:, 1], ACT.Sqrt).then_inc(root_ready, 1)

        @block.vector
        def _(dve):
            chain = [0]

            def link(ins):
                chain[0] += 1
                ins.then_inc(dve_chain, 1)
                dve.wait_ge(dve_chain, chain[0])

            def split(dst, hi, src, lows):
                return dve.scalar_tensor_tensor(dst, hi.bitcast(f32), lows, src, ALU.mult, ALU.add)

            for k in range(COPIES):
                dve.memset(lo_w[k * C:(k + 1) * C, :], -1.0 if k >= COPIES // 2 else 0.0)
            link(dve.memset(ones_r[:, :].bitcast(f32), 0.0))
            link(dve.memset(tri_b[:, :].bitcast(f32), 0.0))
            link(dve.memset(ones_r[0:2, :].bitcast(f32), 1.0))
            dve.wait_ge(ident_made, 1)
            link(dve.tensor_copy(ident_r[:, :], ident[:, 0:N]))
            dve.tensor_reduce(members[:, :], ident[:, :].rearrange("p (c f) -> p f c", f=GROUP), AX.X,
                              ALU.add).then_inc(consts_made, 1)
            dve.tensor_reduce(per_member[:, :], ident[:, :].rearrange("p (f c) -> p f c", f=GROUP), AX.X, ALU.add)
            link(dve.tensor_reduce(per_channel[:, :], ident[:, :].rearrange("p (f c) -> p c f", f=GROUP), AX.X, ALU.add))
            link(dve.tensor_scalar(per_member[:, :], per_member[:, :], 1.0 / C, None, ALU.mult))
            dve.tensor_scalar(averaging[:, :, :], per_channel[:, None, :].to_broadcast([P, GROUP, C]), 1.0 / TOKENS,
                              None, ALU.mult).then_inc(consts_made, 1)
            dve.tensor_tensor(centering[:, :, :], ident[:, :].rearrange("p (f c) -> p c f", f=GROUP),
                              per_member[:, None, :].to_broadcast([P, C, GROUP]), ALU.subtract).then_inc(consts_made, 1)
            dve.tensor_scalar(lo_row[:, :], ident[0:2, 1:2], -1.0, None, ALU.mult)
            link(dve.memset(ident_r[N:P, :].bitcast(f32), 0.0))
            dve.memset(ident_r[N:N + 2, :].bitcast(f32), 1.0).then_inc(consts_made, 1)

            def norm_front(src, layer):
                def by_channel(n):
                    return stat[:, QUADS + n:QUADS + n + 1]

                dve.wait_ge(raw_copied, QUADS * (layer + 1))
                dve.tensor_reduce(by_channel(0), stat[:, 0:QUADS], AX.X, ALU.add).then_inc(chan_total, 1)
                dve.wait_ge(chan_mm, 2 * layer + 1)
                dve.tensor_scalar(by_channel(1), bank_stat[:, 0:1], -1.0, None, ALU.mult).then_inc(mean_ready, 1)
                dve.wait_ge(mean_ready, layer + 1)
                dve.tensor_scalar(centered_t, raw_t, by_channel(1), None, ALU.add).then_inc(chan_centered, 1)
                dve.wait_ge(chan_mm, 2 * layer + 2)
                dve.tensor_scalar(by_channel(3), bank_stat[:, 1:2], EPS, None, ALU.add).then_inc(var_ready, 1)
                dve.wait_ge(root_ready, 2 * layer + 1)
                link(dve.reciprocal(by_channel(5), by_channel(4)))
                dve.tensor_scalar(centering_r[:, :, :], centering[:, :, :], by_channel(5), None,
                                  ALU.mult).then_inc(centering_ready, 1)
                if not layer:
                    weight_stacks()
                else:
                    z_preparation()
                for q in range(QUADS):
                    at = slice(4 * q, 4 * q + 4)
                    dve.wait_ge(d_squared, QUADS * layer + q + 1)
                    ins = dve.tensor_reduce(tok[:, 0, at], squared_d[:, at].rearrange("j b c f -> j b f c"),
                                            AX.X, ALU.add)
                link(ins)
                inverse_root(2 * layer + 1)
                for q in range(QUADS):
                    at = slice(4 * q, 4 * q + 4)
                    dve.tensor_tensor(blocks_t[:, at], banks[q][0:N, :].rearrange("j (b c f) -> j b c f", c=C, f=GROUP),
                                      tok[:, 3, at].unsqueeze(2).to_broadcast([N, 4, C, GROUP]),
                                      ALU.mult).then_inc(normed, 1)

            def inverse_root(before):
                dve.tensor_scalar(tok[:, 1], tok[:, 0], 1.0 / C, EPS, ALU.mult, ALU.add).then_inc(var_ready, 1)
                dve.wait_ge(root_ready, before + 1)
                link(dve.reciprocal(tok[:, 3], tok[:, 2]))

            def z_preparation():
                dve.scalar_tensor_tensor(z_centering.rearrange("p (c f) -> p c f", f=GROUP),
                                         members[:, None, :].to_broadcast([P, C, GROUP]), -1.0 / C,
                                         ident[:, :].rearrange("p (c f) -> p c f", f=GROUP), ALU.mult, ALU.add)
                dve.tensor_scalar(z_scaled, tri_z[:, :, :].rearrange("p f c -> p (f c)"), gb[:, 4:5], None, ALU.mult)
                dve.tensor_copy(beta_wide, gb[:, 5:6].to_broadcast([P, N])).then_inc(z_prepared, 1)

            def weight_stacks():
                dve.wait_ge(prep_copied, 1)
                link(dve.tensor_copy(w_hi[:, :], w_all[:, 0:3 * HD]))
                for n, dst in enumerate((wa_st, wv_st, wg_st)):
                    to = dst[:, :] if n else dst[:, :].rearrange("p (c h) -> p h c", h=H)
                    hi, w = (t[:, n * HD:(n + 1) * HD] for t in (w_hi, w_all))
                    if not n:
                        hi, w = (v.rearrange("p (h c) -> p h c", h=H) for v in (hi, w))
                    split(to, hi, w, lo_w[:, 0:1]).then_inc(stacks_made, 1)

            def chunk(n):
                return slice(n * CB, (n + 1) * CB)

            def tri_deviations():
                for n in range(TRI_BANKS):
                    dve.wait_ge(tri_copied, n + 1)
                    ins = dve.tensor_reduce(tri_sums[:, n].rearrange("j (b f) -> j b f", f=GROUP),
                                            tri_t[:, :, n * GROUP:(n + 1) * GROUP, :].rearrange("j b c f -> j b f c"),
                                            AX.X, ALU.add)
                link(ins)
                link(dve.tensor_reduce(tok[:, 3].rearrange("j b f -> j (b f)"), tri_sums.rearrange("j n t -> j t n"),
                                       AX.X, ALU.add))
                dve.tensor_scalar(tok[:, 1], tok[:, 3], 1.0 / C, None, ALU.mult).then_inc(tri_mean_ready, 1)
                dve.wait_ge(tri_mean_ready, 1)
                for n in range(CHUNKS // 2):
                    center_chunk(dve, n).then_inc(centered, 1)
                for n in range(CHUNKS):
                    dve.wait_ge(squared, n + 1)
                    ins = dve.tensor_reduce(tok[:, 0, chunk(n)],
                                            tri_squares[:, chunk(n)].rearrange("j b c f -> j b f c"), AX.X, ALU.add)
                link(ins)
                dve.tensor_scalar(tok[:, 1], tok[:, 0], 1.0 / C, EPS, ALU.mult, ALU.add).then_inc(var_ready, 1)
                dve.wait_ge(root_ready, 5)
                dve.reciprocal(tok[:, 3], tok[:, 2]).then_inc(root_inverted, 1)
                dve.wait_ge(root_inverted, 1)

            norm_front(xt, 0)
            for b in range(QUADS):
                at = slice(4 * b, 4 * b + 4)
                dve.wait_ge(x_t_ready, b + 1)
                link(dve.tensor_copy(x_parts[:, 0, at, :].bitcast(f32r), x_t[:, at, :]))
                dve.tensor_tensor(x_parts[:, 1, at, :].bitcast(f32r), x_t[:, at, :], x_parts[:, 0, at, :],
                                  ALU.subtract).then_inc(parts_ready, 1)
            dve.wait_ge(weights2_loaded, WEIGHT2_DMAS)
            link(dve.tensor_copy(rows_hi[:, :], rows_in[:, :]))
            dve.wait_ge(tri_stack_copied, 1)
            link(dve.tensor_copy(w_hi[:, 0:PW], w_all[:, 0:PW]))
            split(tri_st[:, :], w_hi[:, 0:PW], w_all[:, 0:PW], lo_w[:, 0:1]).then_inc(tri_stack_made, 1)
            split(tri_b[0:2, :], rows_hi[:, :], rows_in[:, :], lo_row[:, 0:1]).then_inc(rows_split, 1)

            def low_part(g, p):
                dve.wait_ge(u_hi, g + 1)
                dve.tensor_tensor(u_split[:, p, 1], bank_ug[:, 0:GN], u_split[:, p, 0].bitcast(f32),
                                  ALU.subtract).then_inc(u_lo, 1)

            low_part(0, 0)
            low_part(1, 1)
            dve.wait_ge(bias_spread, 16 * H)
            dve.wait_ge(zeroed, ZEROED)
            link(dve.tensor_copy(bias_hi[0:N], pair_bias[:, :, :]))
            dve.tensor_tensor(bias_lo[0:N, 0, 0], pair_bias[:, :, :], bias_hi[0:N].bitcast(f32),
                              ALU.subtract).then_inc(bias_ready, 1)
            dve.wait_ge(bias_ready, 1)
            dve.tensor_copy(bias_lo[0:N, 0, 1:GROUP],
                            bias_lo[0:N, 0, 0:1].bitcast(f32).to_broadcast([N, GROUP - 1, H, N])).then_inc(bias_ready, 1)

            def minus_max(r, m):
                dve.wait_ge(scores_done, BODY * r + m + 1)
                dve.tensor_reduce(neg_max[:, m % BODY, :],
                                  bank_s[m % 4][0:N, 0:H * N].rearrange("p (h k) -> p h k", h=H),
                                  AX.X, ALU.max, negate=True).then_inc(max_ready, 1)

            def step_dve(r, m):
                s = BODY * r + m
                n = m % GROUP
                if live(r, m + 1):
                    minus_max(r, m + 1)
                if n == 0 and live(r, m + 2 * GROUP):
                    low_part(group(r, m) + 2, par(m))
                if n == 1 and live(r, m):
                    g = group(r, m)
                    dve.wait_ge(v_done, g + 1)
                    need(dve, pv_done, GROUP * g - GROUP)
                    dve.tensor_copy(v_sb[0:N, par(m)].rearrange("p i c -> p (i c)"),
                                    bank_v[0:N, :]).then_inc(v_ready, 1)
                if n == 2 and live(r, m - 1 - Y_AFTER):
                    g = group(r, m - 1 - Y_AFTER)
                    dve.wait_ge(y_done, g + 1)
                    dve.wait_ge(g_ready, min(g + 3, BLOCKS) if isinstance(r, int) else g + 3)
                    dve.wait_ge(biased, CHUNKS)
                    rows = res[:, bass.ds(g, 1)].rearrange("p b f c -> p (b f c)")
                    dve.tensor_tensor(rows, bank_ug[0:N, GN:BANK], rows, ALU.add).then_inc(y_added, 1)
                if live(r, m - T_BEHIND):
                    dve.wait_ge(t_done, s - T_BEHIND + 1)
                    need(dve, pv_done, s - T_BEHIND - 1)
                    dve.tensor_copy(probs_t[0:N, (m - T_BEHIND) % 2].rearrange("p h q -> p (h q)"),
                                    bank_t[0:N, 0:H * N]).then_inc(t_ready, 1)
                if live(r, m - 1):
                    dve.wait_ge(exp_done, s)
                    at = (m - 1) % BODY
                    dve.reciprocal(rden[:, at, :], den[:, at, :]).then_inc(rden_ready, 1)
                if n == 3 and live(r, m - GROUP):
                    g, p = group(r, m - GROUP), par(m - GROUP)
                    dve.wait_ge(pv_done, GROUP * g + GROUP)
                    dve.wait_ge(g_ready, g + 1)
                    dve.scalar_tensor_tensor(o_sb[:, p].rearrange("p i q -> p (i q)"),
                                             g_sb[:, p].rearrange("p i q -> p (i q)"), 1.0, bank_o[:, 0:GN],
                                             ALU.add, ALU.mult).then_inc(o_ready, 1)

            minus_max(0, 0)
            run_steps(dve, step_dve)

            dve.wait_ge(y_added, BLOCKS)
            norm_front(res, 1)
            dve.wait_ge(prep2_copied, 1)
            def mask_gates(b):
                dve.wait_ge(gates_ready, 2 * b + 1)
                need(dve, ab_ready, b - 2)
                dve.tensor_tensor(masked[:, b % 3], gates_ab[:, b % 3],
                                  mask1_t[:, :].rearrange("p (f b) -> p f b", f=GROUP)[:, :, b:b + 1]
                                  .to_broadcast([N, GROUP, VALUES * C]), ALU.mult).then_inc(gates_masked, 1)

            mask_gates(0)
            for b in range(BLOCKS):
                if b + 1 < BLOCKS:
                    mask_gates(b + 1)
                dve.wait_ge(gates_ready, 2 * b + 2)
                dve.wait_ge(gates_masked, b + 1)
                dve.tensor_tensor(
                    ab.rearrange("k t h (a f b) -> k a f (t h) b", a=2, f=2)[:, :, :, :, b],
                    projections(b, slice(GATES * C, PW)),
                    masked[:, b % 3].rearrange("k (a f) c -> k a f c", a=2), ALU.mult).then_inc(ab_ready, 1)
            tri_deviations()
            dve.wait_ge(const_gated, 2 * QUADS)
            link(scale_gates(dve, 0))
            for q in range(QUADS):
                at = slice(4 * q, 4 * q + 4)
                dve.wait_ge(z_done, q + 1)
                need(dve, gate_scaled, q)
                link(dve.tensor_tensor(square[:, at],
                                       z_bank(q)[0:N, :].rearrange("p (b f c) -> p b f c", f=GROUP, c=C),
                                       gate_sb[:, at], ALU.mult))
                dve.tensor_tensor(square[:, at], square[:, at], res[:, at], ALU.add).then_inc(out_ready, 1)

        @block.tensor
        def _(pe):
            pe.wait_ge(ident_made, 1)

            def fourfold(bank, at, w, moving):
                for k in range(COPIES):
                    mm = pe.matmul(bank[k * C:(k + 1) * C, at], w, moving, start=True, stop=True)
                return mm

            def wide(w):
                return w.rearrange("p c f -> p (c f)")

            def raw_transposes(src, q, layer):
                for n in range(4):
                    mm = pe.transpose(banks[raw_bank(q, layer)][:, n * N:(n + 1) * N],
                                      src[:, 4 * q + n].rearrange("j f c -> j (f c)"), ident[0:N, 0:N])
                mm.then_inc(raw_transposed, 1)

            def norm_front(src, layer):
                for q in range(layer and RAW_EARLY, QUADS):
                    raw_transposes(src, q, layer)
                mean = averaging[:, :, :].rearrange("p f c -> p (f c)")
                pe.wait_ge(chan_total, layer + 1)
                pe.matmul(bank_stat[:, 0:1], mean, stat[:, QUADS:QUADS + 1], start=True, stop=True).then_inc(chan_mm, 1)
                if not layer:
                    first_weights()
                pe.wait_ge(chan_squared, layer + 1)
                pe.matmul(bank_stat[:, 1:2], mean, stat[:, QUADS + 2:QUADS + 3],
                          start=True, stop=True).then_inc(chan_mm, 1)
                if not layer:
                    second_weights()
                pe.wait_ge(centering_ready, layer + 1)
                for q in range(QUADS):
                    for n in range(4):
                        mm = pe.matmul(banks[q][0:N, n * HD:(n + 1) * HD], centered_t[:, 4 * q + n, :],
                                       centering_r[:, :, :].rearrange("p c f -> p (c f)"), start=True, stop=True)
                    mm.then_inc(d_done, 1)
                if layer:
                    pe.wait_ge(z_prepared, 1)
                    z_weights = tri_z[:, :, :].rearrange("p f c -> p (f c)")
                    pe.matmul(bank_w[:, 0:HD], z_centering, z_scaled, start=True, stop=True)
                    pe.matmul(bank_w[0:N, HD:2 * HD], ones_r[:, :],
                              tri_b[:, None, PW:PW + C].to_broadcast([P, GROUP, C]), start=True, stop=False)
                    pe.matmul(bank_w[0:N, HD:2 * HD], beta_wide, z_weights, start=False, stop=True).then_inc(z_prep_mm, 1)

            def block_transposes(q, layer, read):
                pe.wait_ge(normed, QUADS * layer + q + 1)
                need(pe, read, q - 1)
                if layer and q == 1:
                    pe.wait_ge(z_prep_copied, 1)
                for n in range(4):
                    mm = pe.transpose(banks[6 + q % 2][:, n * N:(n + 1) * N],
                                      blocks_t[:, 4 * q + n].rearrange("p c f -> p (c f)"), ident[0:N, 0:N])
                mm.then_inc(transposed, 1)

            def first_weights():
                pe.wait_ge(weights_loaded, WEIGHT_DMAS)
                pe.wait_ge(wq_scaled, 1)
                for h in range(H):
                    fourfold(bank_w, slice(h * C, (h + 1) * C), wk_in[:, h, :], wq_in[:, h, :])
                fourfold(bank_w, slice(HD, 2 * HD), wv_in[:, :], ident[:, :])
                fourfold(bank_w, slice(2 * HD, 3 * HD), wg_in[:, :], ident[:, :])
                pe.wait_ge(widened, 1)
                pe.transpose(bank_w[:, 3 * HD:3 * HD + H], wide(w_wide[0:H]), ident[0:H, 0:H])
                pe.transpose(bank_w[:, 3 * HD + H:3 * HD + H + 6], wide(norm_wide[:, :, :]), ident[0:6, 0:6])
                pe.transpose(bank_w[:, 3 * HD + H + 6:W_ALL], wo_in[:, :], ident[0:C, 0:C]).then_inc(prep_mm, 1)

            def second_weights():
                pe.wait_ge(prep_copied, 1)
                for n, (at, rows) in enumerate(((0, HD), (HD, C), (HD + C, C))):
                    pe.wait_ge(widened, n + 2)
                    pe.transpose(bank_w[:, at:at + rows], wide(w_wide2[0:rows, n]), ident[0:rows, 0:rows])
                pe.transpose(bank_w[0:N, PW + C:PW + C + N], mask1_in[:, :], ident[0:N, 0:N]).then_inc(prep2_mm, 1)

            pe.wait_ge(consts_made, CONSTS)
            for f in range(GROUP):
                pe.wait_ge(x_loaded[f], 16)
            norm_front(xt, 0)
            pe.wait_ge(prep2_copied, 1)
            fourfold(bank_w, slice(0, HD), tri_in[:, :], ident[:, :])
            fourfold(bank_w, slice(HD, PW), tri_in2[:, :], ident[0:C, 0:C]).then_inc(tri_stack_mm, 1)
            pe.wait_ge(tri_stack_copied, 1)
            for b in range(QUADS + BIAS_AFTER - 1):
                if b < QUADS:
                    block_transposes(b, 0, x_t_ready)
                q = b - BIAS_AFTER + 1
                if q >= 0:
                    pe.wait_ge(x_t_ready, q + 1)
                    if not q:
                        pe.wait_ge(scales_ready, 1)
                    pe.matmul(banks[q][0:GROUP * H, 0:GN], wb_diag[:, :, :].rearrange("p h f -> p (h f)"),
                              x_t[:, 4 * q:4 * q + 4, :].rearrange("p b j -> p (b j)"),
                              start=True, stop=True).then_inc(bias_mm, 1)

            def x_block(g):
                return x_stack[:, :, bass.ds(g, 1), :].rearrange("p f b j -> p f (b j)")

            def u_projection(g):
                need(pe, u_lo, g)
                need(pe, g_ready, g - 2)
                pe.matmul(bank_ug[:, 0:GN], wa_st[:, :], x_block(g), start=True, stop=True).then_inc(u_done, 1)

            def scores_of(r, m):
                g, p, i = group(r, m), par(m), m % GROUP
                if i == 0:
                    pe.wait_ge(staged[p], 16 * STAGED * uses(r, m))
                need(pe, exp_done, BODY * r + m - 3)
                scores = bank_s[m % 4][0:N, 0:H * N]
                pe.matmul(scores, xs[:, p, i, :], u_st[:, p, :, i, :], start=True, stop=False)
                pe.matmul(scores, ident_r[:, :], bias_hi[:, :, :].rearrange("p h k -> p (h k)"),
                          start=False, stop=False)
                pe.matmul(scores, ident_r[:, :], bias_lo[:, p, i].rearrange("p h k -> p (h k)"),
                          start=False, stop=True).then_inc(scores_done, 1)

            def step_pe(r, m):
                s = BODY * r + m
                n = m % GROUP
                if live(r, m + S_AHEAD):
                    scores_of(r, m + S_AHEAD)
                if isinstance(r, int) and N <= s < N + RAW_EARLY:
                    pe.wait_ge(exp_done, s - 3)
                    pe.wait_ge(y_added, 4 * (s - N) + 4)
                    raw_transposes(res, s - N, 1)
                if n == 0 and live(r, m):
                    g, p = group(r, m), par(m)
                    need(pe, v_ready, g)
                    for i in range(GROUP):
                        mm = pe.matmul(bank_v[0:N, i * HD:(i + 1) * HD], xs[:, p, i, :], wv_st[:, :],
                                       start=True, stop=True)
                    mm.then_inc(v_done, 1)
                if n == 1 and live(r, m - Y_AFTER):
                    g, p = group(r, m - Y_AFTER), par(m - Y_AFTER)
                    pe.wait_ge(o_ready, g + 1)
                    pe.wait_ge(u_lo, min(g + 5, BLOCKS) if isinstance(r, int) else g + 5)
                    pe.wait_ge(g_ready, min(g + 2, BLOCKS) if isinstance(r, int) else g + 2)
                    need(pe, y_added, g)
                    for i in range(GROUP):
                        mm = pe.matmul(bank_ug[0:N, GN + i * C:GN + (i + 1) * C], o_sb[:, p, i, :], wo_t[:, :],
                                       start=True, stop=True)
                    mm.then_inc(y_done, 1)
                if n == 1 and live(r, m):
                    g = group(r, m)
                    pe.wait_ge(u_lo, min(g + 3, BLOCKS) if isinstance(r, int) else g + 3)
                    need(pe, g_ready, g)
                    pe.matmul(bank_ug[:, 0:GN], wg_st[:, :], x_block(g), start=True, stop=True).then_inc(g_done, 1)
                if n == 3 and live(r, m + U_AHEAD * GROUP):
                    if m > GROUP:
                        pe.wait_ge(stacked_more, 16 * COPIES * (r + 1))
                    if live(r, m - 2 - Y_AFTER):
                        pe.wait_ge(y_added, group(r, m - 2 - Y_AFTER) + 1)
                    u_projection(group(r, m) + U_AHEAD)
                if live(r, m - T_BEHIND):
                    pe.wait_ge(probs_ready, s - T_BEHIND + 1)
                    need(pe, t_ready, s - T_BEHIND)
                    for h in range(H):
                        mm = pe.transpose(bank_t[0:N, h * N:(h + 1) * N], probs[:, (m - T_BEHIND) % SLOTS, h, :],
                                          ident[0:N, 0:N])
                    mm.then_inc(t_done, 1)
                if live(r, m - PV_BEHIND):
                    j = m - PV_BEHIND
                    g, p, i = group(r, j), par(j), j % GROUP
                    pe.wait_ge(t_ready, s - PV_BEHIND + 1)
                    if i == 0:
                        pe.wait_ge(v_ready, g + 1)
                        need(pe, o_ready, g)
                    for h in range(H):
                        mm = pe.matmul(bank_o[h * C:(h + 1) * C, i * N:(i + 1) * N],
                                       v_sb[:, p, i, h * C:(h + 1) * C], probs_t[:, j % 2, h, :],
                                       start=True, stop=True)
                    mm.then_inc(pv_done, 1)

            pe.wait_ge(stacked, 16 * COPIES)
            pe.wait_ge(stacks_made, 3)
            u_projection(0)
            u_projection(1)
            pe.wait_ge(zeroed, ZEROED)
            pe.wait_ge(bias_ready, 1)
            scores_of(0, 0)
            pe.wait_ge(bias_ready, 2)
            scores_of(0, 1)
            u_projection(2)
            pe.wait_ge(bias_copy, 1)
            run_steps(pe, step_pe)

            pe.wait_ge(y_added, BLOCKS)
            norm_front(res, 1)

            def project(b):
                need(pe, ab_ready, b - 3)
                for a in range(2):
                    to = banks[projection_banks(b) + a][0:N, 0:2 * PW]
                    pe.matmul(to, ones_r[:, :], tri_b[:, None, 0:PW].to_broadcast([P, 2, PW]),
                              start=True, stop=False)
                    if b < 4:
                        mm = pe.matmul(to, zn_t[:, b, :], tri_gv[:, 2 * a:2 * a + 2, :].rearrange("p f c -> p (f c)"),
                                       start=False, stop=True)
                    else:
                        for f in range(2):
                            mm = pe.matmul(to[:, f * PW:(f + 1) * PW], x_stack[:, 2 * a + f, b, :], tri_st[:, :],
                                           start=False, stop=f == 1)
                mm.then_inc(proj_done, 1)

            for q in range(ZN_AHEAD):
                block_transposes(q, 1, zn_ready)
            for b in range(BLOCKS):
                if b == 0:
                    pe.wait_ge(zn_ready, 1)
                elif b <= QUADS - ZN_AHEAD:
                    block_transposes(ZN_AHEAD + b - 1, 1, zn_ready)
                if b == 2:
                    pe.wait_ge(normed, 2 * QUADS)
                if b == 3:
                    pe.wait_ge(zn_ready, QUADS)
                if b >= 4 and b % 4 == 0:
                    pe.wait_ge(zn_stacked[b // 4 - 1], 16 * COPIES)
                if b == 4:
                    pe.wait_ge(tri_stack_made, 1)
                project(b)
            pe.wait_ge(ab_ready, BLOCKS)
            for b in range(TRI_BANKS):
                need(pe, tri_copied, b - 3)
                for n in range(GROUP):
                    h = b * GROUP + n
                    mm = pe.matmul(banks[4 + b % 4][0:N, n * N:(n + 1) * N], ab[:, 1, h, :], ab[:, 0, h, :],
                                   start=True, stop=True)
                mm.then_inc(tri_done, 1)
            pe.wait_ge(tri_copied, TRI_BANKS)
            for q in range(QUADS + Z_AFTER):
                if q < QUADS:
                    need(pe, tn_ready, q - 3)
                    for n in range(4):
                        mm = pe.transpose(banks[q % 4][:, n * N:(n + 1) * N],
                                          tri_t[:, 4 * q + n].rearrange("p c f -> p (c f)"), ident[0:N, 0:N])
                    mm.then_inc(block_t, 1)
                z = q - Z_AFTER
                if z >= 0:
                    pe.wait_ge(tn_ready, z + 1)
                    for n in range(4):
                        mm = pe.matmul(z_bank(z)[0:N, n * HD:(n + 1) * HD], tn_t[:, 4 * z + n, :], z_centered,
                                       start=True, stop=True)
                    mm.then_inc(z_done, 1)


_INS = ["x", "L0_conv_mask", "L0_conv_ln_gamma", "L0_conv_ln_beta", "L0_conv_w_bias", "L0_conv_wq",
        "L0_conv_wk", "L0_conv_wv", "L0_conv_wg", "L0_conv_bg", "L0_conv_wo", "L0_conv_bo", "L1_conv_mask",
        "L1_conv_ln_in_w", "L1_conv_ln_in_b", "L1_conv_a_g_w", "L1_conv_a_g_b", "L1_conv_a_p_w",
        "L1_conv_a_p_b", "L1_conv_b_g_w", "L1_conv_b_g_b", "L1_conv_b_p_w", "L1_conv_b_p_b", "L1_conv_g_w",
        "L1_conv_g_b", "L1_conv_ln_out_w", "L1_conv_ln_out_b", "L1_conv_z_w", "L1_conv_z_b"]


def kernel(**inputs):
    import numpy as _np
    import concourse.bacc as _bacc
    from concourse import mybir as _mybir
    from concourse.bass_utils import run_bass_kernel_spmd as _run

    nc = _bacc.Bacc("TRN2", target_bir_lowering=False, num_devices=1)
    arrays, args = {}, []
    for name in _INS:
        a = _np.ascontiguousarray(inputs[name])
        arrays[f"in_{name}"] = a
        args.append(nc.dram_tensor(f"in_{name}", a.shape, _mybir.dt.from_np(a.dtype), kind="ExternalInput").ap())
    args.append(nc.dram_tensor("out_y", inputs["x"].shape, _mybir.dt.float32, kind="ExternalOutput").ap())
    triangle_kernel(nc, *args)
    r = _run(nc, [arrays], core_ids=[0])
    return r.results[0]["out_y"]
```
